# Optimizing a Trainium2 kernel written in Bass

```python
import numpy as np
import jax
import jax.numpy as jnp

def _softmax(x, axis=-1):
    return jax.nn.softmax(x, axis=axis)

def _gelu(x):
    return jax.nn.gelu(x, approximate=True)

def _silu(x):
    return jax.nn.silu(x)

def _sigmoid(x):
    return jax.nn.sigmoid(x)

def _layernorm(x, axis=-1, eps=1e-05):
    m = jnp.mean(x, axis=axis, keepdims=True)
    v = jnp.var(x, axis=axis, keepdims=True)
    return (x - m) / jnp.sqrt(v + eps)

def _scatter_add(tgt, idx, src, axis=0):
    return tgt.at[idx].add(src)

def _segment_sum(src, seg, n):
    return jax.ops.segment_sum(src, seg, n)
kernel_name = 'mk_adj_seq_d4_adj_r2_a514d2'

def setup_inputs(seed: int=0):
    np.random.seed(seed)
    _w = jnp.asarray

    def _rec_inputs():
        import jax
        import jax.numpy as jnp
        _gk = jax.random.key(seed)
        x = -0.0002928 + 1 * jax.random.normal(jax.random.fold_in(_gk, 1), (64, 128, 256), jnp.float32)
        _a = jax.random.bernoulli(jax.random.fold_in(_gk, 2), 0.125, (64, 128, 128))
        _a = jnp.logical_or(_a, jnp.swapaxes(_a, -1, -2))
        _a = jnp.logical_or(_a, jnp.eye(128, dtype=bool))
        _af = _a.astype(jnp.float32)
        _af = _af / jnp.maximum(_af.sum(-1, keepdims=True), 1.0)
        adj = _af
        return (x, adj)
    x, adj = _rec_inputs()

    def _L0_gnn_setup():
        import jax, jax.numpy as jnp
        import numpy as np
        B, N, D, H = (8, 512, 256, 8)
        DK = D // H
        LN_EPS = 1e-05
        ADJ_MIN = 1e-08

        def _layer_norm(x, gamma, beta):
            mu = jnp.mean(x, axis=-1, keepdims=True)
            var = jnp.mean(jnp.square(x - mu), axis=-1, keepdims=True)
            return (x - mu) * jax.lax.rsqrt(var + LN_EPS) * gamma + beta
        key = jax.random.key(seed)
        ks = jax.random.split(key, 12)
        x = jax.random.normal(ks[0], (B, N, D), dtype=jnp.float32)
        adj = jax.random.uniform(ks[1], (B, N, N), dtype=jnp.float32)
        adj = adj / jnp.sum(adj, axis=-1, keepdims=True)
        s = 1.0 / np.sqrt(D)
        Wq = jax.random.normal(ks[2], (D, D), dtype=jnp.float32) * s
        bq = jnp.zeros((D,), dtype=jnp.float32)
        Wk = jax.random.normal(ks[3], (D, D), dtype=jnp.float32) * s
        bk = jnp.zeros((D,), dtype=jnp.float32)
        Wv = jax.random.normal(ks[4], (D, D), dtype=jnp.float32) * s
        bv = jnp.zeros((D,), dtype=jnp.float32)
        Wo = jax.random.normal(ks[5], (D, D), dtype=jnp.float32) * s
        bo = jnp.zeros((D,), dtype=jnp.float32)
        gamma = jnp.ones((D,), dtype=jnp.float32)
        beta = jnp.zeros((D,), dtype=jnp.float32)
        return {'x': x, 'adj': adj, 'Wq': Wq, 'bq': bq, 'Wk': Wk, 'bk': bk, 'Wv': Wv, 'bv': bv, 'Wo': Wo, 'bo': bo, 'gamma': gamma, 'beta': beta}
    _L0_gnn_all = _L0_gnn_setup()
    _L0_gnn_in = {k: v for k, v in _L0_gnn_all.items() if k in ('Wq', 'bq', 'Wk', 'bk', 'Wv', 'bv', 'Wo', 'bo', 'gamma', 'beta')}
    del _L0_gnn_all

    def _L1_gnn_setup():
        import jax, jax.numpy as jnp
        import numpy as np
        BS, N, H = (8, 1024, 256)
        NEG_INF = -1000000000.0
        LEAKY_SLOPE = 0.01
        key = jax.random.key(seed)
        ks = jax.random.split(key, 8)
        feats = jax.random.normal(ks[0], (BS, N, H), dtype=jnp.float32)
        adj = jax.random.randint(ks[1], (BS, N, N), 0, 2).astype(jnp.float32)
        adj = jnp.maximum(adj, jnp.eye(N, dtype=jnp.float32)[None])
        s = 1.0 / np.sqrt(H)
        return {'feats': feats, 'adj_mat': adj, 'fc_w': jax.random.normal(ks[2], (H, H), dtype=jnp.float32) * s, 'fc_b': jax.random.normal(ks[3], (H,), dtype=jnp.float32) * s, 'q_w': jax.random.normal(ks[4], (1, H), dtype=jnp.float32) * s, 'q_b': jax.random.normal(ks[5], (1,), dtype=jnp.float32) * s, 'k_w': jax.random.normal(ks[6], (1, H), dtype=jnp.float32) * s, 'k_b': jax.random.normal(ks[7], (1,), dtype=jnp.float32) * s}
    _L1_gnn_all = _L1_gnn_setup()
    _L1_gnn_in = {k: v for k, v in _L1_gnn_all.items() if k in ('fc_w', 'fc_b', 'q_w', 'q_b', 'k_w', 'k_b')}
    del _L1_gnn_all

    def _L2_gnn_setup():
        import jax, jax.numpy as jnp
        import numpy as np
        NUM_HEADS = 8
        EPS = 1e-09
        key = jax.random.key(seed)
        ks = jax.random.split(key, 8)
        B, N, D = (2, 1024, 256)
        s = 1.0 / np.sqrt(D)
        x = jax.random.normal(ks[0], (B, N, D), dtype=jnp.float32)
        adjacency = jax.random.uniform(ks[1], (B, N, N), dtype=jnp.float32)
        W_q = jax.random.normal(ks[2], (D, D), dtype=jnp.float32) * s
        W_k = jax.random.normal(ks[3], (D, D), dtype=jnp.float32) * s
        W_v = jax.random.normal(ks[4], (D, D), dtype=jnp.float32) * s
        b_q = jnp.zeros((D,), jnp.float32)
        b_k = jnp.zeros((D,), jnp.float32)
        b_v = jnp.zeros((D,), jnp.float32)
        w_g = jax.random.normal(ks[5], (2 * D,), dtype=jnp.float32) * (1.0 / np.sqrt(2 * D))
        b_g = jnp.zeros((), jnp.float32)
        return {'x': x, 'adjacency': adjacency, 'W_q': W_q, 'b_q': b_q, 'W_k': W_k, 'b_k': b_k, 'W_v': W_v, 'b_v': b_v, 'w_g': w_g, 'b_g': b_g}
    _L2_gnn_all = _L2_gnn_setup()
    _L2_gnn_in = {k: v for k, v in _L2_gnn_all.items() if k in ('W_q', 'b_q', 'W_k', 'b_k', 'W_v', 'b_v', 'w_g', 'b_g')}
    del _L2_gnn_all

    def _L3_gnn_setup():
        import jax, jax.numpy as jnp
        import numpy as np
        NUM_HID = 256
        BS, N = (8, 1024)
        NEG_BIG = -1000000000.0
        LEAKY_SLOPE = 0.01
        key = jax.random.key(seed)
        k_feats, k_adj, k_w, k_wq, k_wk = jax.random.split(key, 5)
        feats = jax.random.normal(k_feats, (BS, N, NUM_HID), dtype=jnp.float32)
        adj = (jax.random.uniform(k_adj, (BS, N, N)) < 0.05).astype(jnp.float32)
        eye = jnp.eye(N, dtype=jnp.float32)[None]
        adj_mat = jnp.maximum(adj, eye)
        s = 1.0 / np.sqrt(NUM_HID)
        W_fc = jax.random.uniform(k_w, (NUM_HID, NUM_HID), minval=-s, maxval=s, dtype=jnp.float32)
        b_fc = jnp.zeros((NUM_HID,), dtype=jnp.float32)
        w_q = jax.random.uniform(k_wq, (NUM_HID, 1), minval=-s, maxval=s, dtype=jnp.float32)
        b_q = jnp.zeros((1,), dtype=jnp.float32)
        w_k = jax.random.uniform(k_wk, (NUM_HID, 1), minval=-s, maxval=s, dtype=jnp.float32)
        b_k = jnp.zeros((1,), dtype=jnp.float32)
        return {'feats': feats, 'adj_mat': adj_mat, 'W_fc': W_fc, 'b_fc': b_fc, 'w_q': w_q, 'b_q': b_q, 'w_k': w_k, 'b_k': b_k}
    _L3_gnn_all = _L3_gnn_setup()
    _L3_gnn_in = {k: v for k, v in _L3_gnn_all.items() if k in ('W_fc', 'b_fc', 'w_q', 'b_q', 'w_k', 'b_k')}
    del _L3_gnn_all
    return {'x': x, 'adj': adj, 'L0_gnn_Wq': _L0_gnn_in['Wq'], 'L0_gnn_bq': _L0_gnn_in['bq'], 'L0_gnn_Wk': _L0_gnn_in['Wk'], 'L0_gnn_bk': _L0_gnn_in['bk'], 'L0_gnn_Wv': _L0_gnn_in['Wv'], 'L0_gnn_bv': _L0_gnn_in['bv'], 'L0_gnn_Wo': _L0_gnn_in['Wo'], 'L0_gnn_bo': _L0_gnn_in['bo'], 'L0_gnn_gamma': _L0_gnn_in['gamma'], 'L0_gnn_beta': _L0_gnn_in['beta'], 'L1_gnn_fc_w': _L1_gnn_in['fc_w'], 'L1_gnn_fc_b': _L1_gnn_in['fc_b'], 'L1_gnn_q_w': _L1_gnn_in['q_w'], 'L1_gnn_q_b': _L1_gnn_in['q_b'], 'L1_gnn_k_w': _L1_gnn_in['k_w'], 'L1_gnn_k_b': _L1_gnn_in['k_b'], 'L2_gnn_W_q': _L2_gnn_in['W_q'], 'L2_gnn_b_q': _L2_gnn_in['b_q'], 'L2_gnn_W_k': _L2_gnn_in['W_k'], 'L2_gnn_b_k': _L2_gnn_in['b_k'], 'L2_gnn_W_v': _L2_gnn_in['W_v'], 'L2_gnn_b_v': _L2_gnn_in['b_v'], 'L2_gnn_w_g': _L2_gnn_in['w_g'], 'L2_gnn_b_g': _L2_gnn_in['b_g'], 'L3_gnn_W_fc': _L3_gnn_in['W_fc'], 'L3_gnn_b_fc': _L3_gnn_in['b_fc'], 'L3_gnn_w_q': _L3_gnn_in['w_q'], 'L3_gnn_b_q': _L3_gnn_in['b_q'], 'L3_gnn_w_k': _L3_gnn_in['w_k'], 'L3_gnn_b_k': _L3_gnn_in['b_k']}

def reference(x, adj, L0_gnn_Wq, L0_gnn_bq, L0_gnn_Wk, L0_gnn_bk, L0_gnn_Wv, L0_gnn_bv, L0_gnn_Wo, L0_gnn_bo, L0_gnn_gamma, L0_gnn_beta, L1_gnn_fc_w, L1_gnn_fc_b, L1_gnn_q_w, L1_gnn_q_b, L1_gnn_k_w, L1_gnn_k_b, L2_gnn_W_q, L2_gnn_b_q, L2_gnn_W_k, L2_gnn_b_k, L2_gnn_W_v, L2_gnn_b_v, L2_gnn_w_g, L2_gnn_b_g, L3_gnn_W_fc, L3_gnn_b_fc, L3_gnn_w_q, L3_gnn_b_q, L3_gnn_w_k, L3_gnn_b_k):
    import jax
    import jax.numpy as jnp

    def _L0_gnn_ref(x, adj, Wq, bq, Wk, bk, Wv, bv, Wo, bo, gamma, beta):
        import jax, jax.numpy as jnp
        import numpy as np
        B, N, D, H = (8, 512, 256, 8)
        DK = D // H
        LN_EPS = 1e-05
        ADJ_MIN = 1e-08

        def _layer_norm(x, gamma, beta):
            mu = jnp.mean(x, axis=-1, keepdims=True)
            var = jnp.mean(jnp.square(x - mu), axis=-1, keepdims=True)
            return (x - mu) * jax.lax.rsqrt(var + LN_EPS) * gamma + beta
        b, n, d = x.shape
        q = (x @ Wq.T + bq).reshape(b, n, H, DK).transpose(0, 2, 1, 3)
        k = (x @ Wk.T + bk).reshape(b, n, H, DK).transpose(0, 2, 1, 3)
        v = (x @ Wv.T + bv).reshape(b, n, H, DK).transpose(0, 2, 1, 3)
        logits = jnp.einsum('bhqd,bhkd->bhqk', q, k) / np.sqrt(DK)
        logits = logits + jnp.log(jnp.clip(adj, ADJ_MIN, None))[:, None, :, :]
        attn = jax.nn.softmax(logits, axis=-1)
        out = jnp.einsum('bhqk,bhkd->bhqd', attn, v)
        out = out.transpose(0, 2, 1, 3).reshape(b, n, d)
        out = out @ Wo.T + bo
        return _layer_norm(x + out, gamma, beta)

    def _L1_gnn_ref(feats, adj_mat, fc_w, fc_b, q_w, q_b, k_w, k_b):
        import jax, jax.numpy as jnp
        import numpy as np
        BS, N, H = (8, 1024, 256)
        NEG_INF = -1000000000.0
        LEAKY_SLOPE = 0.01
        feat_proj = jnp.einsum('bnh,oh->bno', feats, fc_w) + fc_b
        q = jnp.einsum('bnh,oh->bno', feat_proj, q_w) + q_b
        k = jnp.einsum('bnh,oh->bno', feat_proj, k_w) + k_b
        logits = q + jnp.swapaxes(k, 2, 1)
        masked = logits + (1.0 - adj_mat) * NEG_INF
        masked = jnp.where(masked >= 0, masked, LEAKY_SLOPE * masked)
        atten = jax.nn.softmax(masked, axis=-1)
        out = jnp.einsum('bnm,bmh->bnh', atten, feat_proj)
        return out + feats

    def _L2_gnn_ref(x, adjacency, W_q, b_q, W_k, b_k, W_v, b_v, w_g, b_g):
        import jax, jax.numpy as jnp
        import numpy as np
        NUM_HEADS = 8
        EPS = 1e-09
        B, N, D = x.shape
        H = NUM_HEADS
        hd = D // H
        Q = (x @ W_q + b_q).reshape(B, N, H, hd)
        K = (x @ W_k + b_k).reshape(B, N, H, hd)
        V = (x @ W_v + b_v).reshape(B, N, H, hd)
        scores = jnp.einsum('bihd,bjhd->bhij', Q, K) / jnp.sqrt(jnp.float32(hd))
        a = x @ w_g[:D]
        c = x @ w_g[D:]
        soul_bias = a[:, :, None] + c[:, None, :] + b_g
        scores = scores + (soul_bias + jnp.log(adjacency + EPS))[:, None, :, :]
        attn = jax.nn.softmax(scores, axis=-1)
        out = jnp.einsum('bhij,bjhd->bihd', attn, V).reshape(B, N, D)
        return out + x

    def _L3_gnn_ref(feats, adj_mat, W_fc, b_fc, w_q, b_q, w_k, b_k):
        import jax, jax.numpy as jnp
        import numpy as np
        NUM_HID = 256
        BS, N = (8, 1024)
        NEG_BIG = -1000000000.0
        LEAKY_SLOPE = 0.01
        feat_proj = jnp.einsum('bnd,de->bne', feats, W_fc) + b_fc
        q = jnp.einsum('bnd,do->bno', feat_proj, w_q) + b_q
        k = jnp.einsum('bnd,do->bno', feat_proj, w_k) + b_k
        logits = q + jnp.swapaxes(k, 2, 1)
        masked = logits + (1.0 - adj_mat) * NEG_BIG
        masked = jnp.where(masked >= 0, masked, LEAKY_SLOPE * masked)
        atten = jax.nn.softmax(masked, axis=-1)
        out = jnp.einsum('bnm,bmd->bnd', atten, feat_proj)
        return out + feats
    x = _L0_gnn_ref(x, adj, L0_gnn_Wq, L0_gnn_bq, L0_gnn_Wk, L0_gnn_bk, L0_gnn_Wv, L0_gnn_bv, L0_gnn_Wo, L0_gnn_bo, L0_gnn_gamma, L0_gnn_beta)
    x = _L1_gnn_ref(x, adj, L1_gnn_fc_w, L1_gnn_fc_b, L1_gnn_q_w, L1_gnn_q_b, L1_gnn_k_w, L1_gnn_k_b)
    x = _L2_gnn_ref(x, adj, L2_gnn_W_q, L2_gnn_b_q, L2_gnn_W_k, L2_gnn_b_k, L2_gnn_W_v, L2_gnn_b_v, L2_gnn_w_g, L2_gnn_b_g)
    x = _L3_gnn_ref(x, adj, L3_gnn_W_fc, L3_gnn_b_fc, L3_gnn_w_q, L3_gnn_b_q, L3_gnn_w_k, L3_gnn_b_k)
    return x

_drawn_inputs = setup_inputs


def setup_inputs(seed=0):
    import zlib

    import numpy as np

    out = dict(_drawn_inputs(seed))
    spreads = {'L0_gnn_bq': (0.0, 0.1),
     'L0_gnn_bk': (0.0, 2.0),
     'L0_gnn_bv': (0.0, 0.1),
     'L0_gnn_bo': (0.0, 0.1),
     'L0_gnn_gamma': (1.0, 0.2),
     'L0_gnn_beta': (0.0, 0.1),
     'L2_gnn_b_q': (0.0, 0.357),
     'L2_gnn_b_k': (0.0, 2.0),
     'L2_gnn_b_v': (0.0, 0.1),
     'L3_gnn_b_fc': (0.0, 0.1)}
    factors = {'L1_gnn_q_w': 5.802, 'L1_gnn_k_w': 4.489, 'L3_gnn_w_q': 50.508, 'L3_gnn_w_k': 35.907}
    for name, (base, spread) in spreads.items():
        noise = np.random.default_rng([zlib.crc32(name.encode()), seed]).standard_normal(out[name].shape)
        drawn = base * np.exp(spread * noise) if base else spread * noise
        out[name] = jnp.asarray(drawn.astype(out[name].dtype))
    for name, factor in factors.items():
        out[name] = (out[name] * factor).astype(out[name].dtype)
    return out
```

```python
from contextlib import ExitStack

import concourse.bass as bass
from concourse import mybir

FP32 = mybir.dt.float32
FP32R = mybir.dt.float32r
BF16 = mybir.dt.bfloat16
ALU = mybir.AluOpType
ACT = mybir.ActivationFunctionType
AX = mybir.AxisListType

B, N, D, H = 64, 128, 256, 8
DK = D // H
P = 128
KT = D // P
HPT = P // DK
PAIRS = B // 2
PN = 2 * N
DV = DK + 1
DX = D + 2
LATE = 4
CHUNKS = 8
LN_EPS = 1e-05
ADJ_MIN = 1e-08
ADJ_EPS = 1e-09
MASKED = 1e9
LEAKY = 0.01
W_SLOTS = ["q0", "k0", "v0", "o0", "fc1", "q2", "k2", "v2", "fc3"]
B_SLOTS = ["v0", "o0", "fc1", "v2", "fc3"]


def wait(eng, sem, value):
    if isinstance(value, int) and value <= 0:
        return
    eng.wait_ge(sem, value)


def steps(eng, first, last, even_first, even_end, emit):
    for t in range(first, even_first):
        emit(t, t % 2)
    with eng.Fori(even_first, even_end - 1, 2) as t:
        emit(t, 0)
        emit(t + 1, 1)
    for t in range(even_end, last + 1):
        emit(t, t % 2)


def within(t, lo, hi):
    return not isinstance(t, int) or lo <= t < hi


def build(nc, x, adj, weights, fc_rev, qk_w, bias_cols, bias_rows, qk_b, gamma, beta, w_g, b_g, eye, out):
    ctx = ExitStack()
    with ctx:
        def sb(name, shape, dt=FP32):
            return ctx.enter_context(nc.sbuf_tensor(name, shape, dt))

        def sem(name):
            return ctx.enter_context(nc.semaphore(name))

        X = sb("X", [P, B * D])
        ADJ = sb("ADJ", [P, B * N])
        w_hi = sb("w_hi", [P, len(W_SLOTS), KT, DX], FP32R)
        w_lo = sb("w_lo", [P, len(W_SLOTS), KT, DX], FP32R)
        ident = sb("ident", [P, P])
        bcol = sb("bcol", [P, 4, KT])
        brow = sb("brow", [96, len(B_SLOTS), DX], BF16)
        ones3 = sb("ones3", [96, P], BF16)
        gamma_b = sb("gamma_b", [P, D])
        beta_b = sb("beta_b", [P, D])
        xin = sb("xin", [P, 2, 2, D])
        xT_hi = sb("xT_hi", [P, 2, KT, PN], FP32R)
        xT_lo = sb("xT_lo", [P, 2, KT, PN], FP32R)
        QT = sb("QT", [P, 2, KT, PN])
        KBD = sb("KBD", [P, KT, 2, HPT, N])
        V = sb("V", [P, 2, 2, H, DV])
        negmax = sb("negmax", [P, 2, H])
        adjw = sb("adjw", [P, 2, 2, N])
        node_b = sb("node_b", [P, 2, 2, 2])
        log_adj = sb("log_adj", [P, 2, 2, N])
        edge_b = sb("edge_b", [P, 2, 2, N])
        att = sb("att", [P, 2, H, N])
        attT = sb("attT", [P, 2, H, N])
        rsum = sb("rsum", [P, 2, H])
        onorm = sb("onorm", [P, 2, D])
        oT_hi = sb("oT_hi", [P, KT, PN], FP32R)
        oT_lo = sb("oT_lo", [P, KT, PN], FP32R)
        yres = sb("yres", [P, 2, D])
        stats = sb("stats", [P, 2, 6])
        mv = sb("mv", [P, 2, 2])
        veps = sb("veps", [P, 2, 1])
        rstd = sb("rstd", [P, 2, 1])
        mhalf = sb("mhalf", [P, 1])
        eps_col = sb("eps_col", [P, 1])
        ln_eps = sb("ln_eps", [P, 1])
        VX = sb("VX", [P, 2, 2, DX])
        mbias = sb("mbias", [P, 2, N])
        logit = sb("logit", [P, 2, N])
        leaky = sb("leaky", [P, 2, N])
        nmax1 = sb("nmax1", [P, 2])
        prob = sb("prob", [P, 2, N])
        psum1 = sb("psum1", [P, 2])
        prec = sb("prec", [P, 2])
        probT = sb("probT", [P, 2, N])

        bank = [ctx.enter_context(nc.psum_tensor(f"bank{n}", [P, 512], FP32)) for n in range(4)]
        SC = ctx.enter_context(nc.psum_tensor("SC", [P, H, N], FP32))
        AT = ctx.enter_context(nc.psum_tensor("AT", [P, H, N], FP32))
        XO, QK, VY, PV = bank

        load_x = [sem(f"load_x{c}") for c in range(CHUNKS)]
        load_adj = [sem(f"load_adj{c}") for c in range(CHUNKS)]
        load_w = sem("load_w")
        load_c = sem("load_c")
        prep_p = sem("prep_p")
        prep_v = sem("prep_v")
        prep_t = sem("prep_t")
        prepared = sem("prepared")
        stored = sem("stored")
        xfinal = [sem(f"xfinal{l}") for l in range(4)]

        G = B // CHUNKS
        Xg = X[:, :].rearrange("p (g d) -> p g d", d=D)
        Ag = ADJ[:, :].rearrange("p (g n) -> p g n", n=N)

        free_at = [LATE * G * D]

        def early(rows, *shape):
            n = 1
            for s in shape:
                n *= s
            at = free_at[0]
            free_at[0] = at + n
            letters = "abcd"[:len(shape)]
            return X[0:rows, at:at + n].rearrange(f"p ({' '.join(letters)}) -> p {' '.join(letters)}",
                                                  **dict(zip(letters, shape)))

        w_raw = early(P, len(W_SLOTS), KT, D)
        wg_raw = early(P, KT, 2)
        qkw = early(P, 2, KT, 2)
        bfc = early(P, 2, KT)
        qkb = early(96, 2, 2)
        bg = early(96, 1)
        row_raw = early(96, len(B_SLOTS), DX)
        row_res = early(96, len(B_SLOTS), DX)
        fc_raw = att[:, :, :, :].rearrange("p a h n -> p (a h n)")[:, 0:2 * KT * D]\
            .rearrange("p (f t d) -> p f t d", f=2, t=KT)
        row_part = sb("row_part", [96, len(B_SLOTS), DX], BF16)

        def slot(names, name):
            return names.index(name)

        FC = [slot(W_SLOTS, "fc1"), slot(W_SLOTS, "fc3")]
        WV2 = slot(W_SLOTS, "v2")
        FB = [slot(B_SLOTS, "fc1"), slot(B_SLOTS, "fc3")]

        block = ctx.enter_context(nc.Block())
        progs = {"sync": [], "gpsimd": [], "scalar": [], "tensor": [], "vector": []}

        def sync_prep(sp):
            sp.dma_start(w_raw, weights).then_inc(load_w, 16)
            for c in range(CHUNKS):
                if c < LATE:
                    sp.dma_start(Xg[:, G * c:G * (c + 1), :],
                                 x[G * c:G * (c + 1)].rearrange("g p d -> p g d")).then_inc(load_x[c], 16)
                sp.dma_start(Ag[:, G * c:G * (c + 1), :],
                             adj[G * c:G * (c + 1)].rearrange("g p n -> p g n")).then_inc(load_adj[c], 16)

        def scalar_prep(act):
            act.dma_start(ident[:, :], eye).then_inc(load_c, 16)
            act.dma_start(fc_raw, fc_rev).then_inc(load_c, 16)
            act.dma_start(qkw, qk_w).then_inc(load_c, 16)
            act.dma_start(bcol[:, :, :], bias_cols[:, 0:4, :]).then_inc(load_c, 16)
            act.dma_start(bfc, bias_cols[:, 4:6, :]).then_inc(load_c, 16)
            act.dma_start(row_raw[:, :, 0:D], bias_rows.partition_broadcast(96)).then_inc(load_c, 16)
            act.dma_start(qkb, qk_b.partition_broadcast(96)).then_inc(load_c, 16)
            act.dma_start(gamma_b[:, :], gamma.partition_broadcast(P)).then_inc(load_c, 16)
            act.dma_start(beta_b[:, :], beta.partition_broadcast(P)).then_inc(load_c, 16)
            act.dma_start(wg_raw, w_g).then_inc(load_c, 16)
            act.dma_start(bg, b_g.partition_broadcast(96)).then_inc(load_c, 16)
            act.wait_ge(load_c, 11 * 16)
            for s in (0, 2):
                nc.scalar.mul(bcol[:, s, :], bcol[:, s, :], float(DK) ** -0.5).then_inc(prepared, 1)
            act.wait_ge(prepared, PREPARED)
            for c in range(LATE, CHUNKS):
                act.dma_start(Xg[:, G * c:G * (c + 1), :],
                              x[G * c:G * (c + 1)].rearrange("g p d -> p g d")).then_inc(load_x[c], 16)

        def gpsimd_prep(pool):
            nc.gpsimd.memset(KBD[:, :, :, :, :], 0.0).then_inc(prepared, 1)
            nc.gpsimd.memset(V[:, :, :, :, DK:DV], 1.0).then_inc(prepared, 1)
            nc.gpsimd.memset(mhalf[:, :], -0.5).then_inc(prepared, 1)
            nc.gpsimd.memset(eps_col[:, :], ADJ_EPS).then_inc(prepared, 1)
            nc.gpsimd.memset(ln_eps[:, :], LN_EPS).then_inc(prepared, 1)
            nc.gpsimd.memset(row_raw[:, :, D:DX], 0.0).then_inc(prep_p, 1)
            nc.gpsimd.memset(ones3[:, :], 0.0).then_inc(prep_p, 1)
            pool.wait_ge(prep_p, 2)
            for r in (0, 32, 64):
                nc.gpsimd.memset(ones3[r:r + 1, :], 1.0).then_inc(prepared, 1)

        def tensor_prep(pe):
            pe.wait_ge(load_c, 11 * 16)
            for f in range(2):
                for m in range(KT):
                    for t in range(KT):
                        mm = nc.tensor.matmul(PV[:, 4 * f + 2 * m:4 * f + 2 * m + 2],
                                              fc_raw[:, f, t, m * P:(m + 1) * P], qkw[:, f, t, :],
                                              start=(t == 0), stop=(t == KT - 1))
            mm.then_inc(prep_t, 1)
            for f in range(2):
                for t in range(KT):
                    mm = nc.tensor.matmul(VY[0:96, 2 * f:2 * f + 2],
                                          bfc[:, f, t:t + 1].broadcast_to([P, 96]), qkw[:, f, t, :],
                                          start=(t == 0), stop=(t == KT - 1))
            mm.then_inc(prep_t, 1)

        def vector_prep(dve):
            dve.wait_ge(load_w, 16)
            nc.vector.tensor_copy(w_hi[:, :, :, 0:D], w_raw).then_inc(prep_v, 1)
            dve.wait_ge(prep_v, 1)
            nc.vector.tensor_tensor(w_lo[:, :, :, 0:D], w_raw,
                                    w_hi[:, :, :, 0:D].bitcast(FP32), ALU.subtract).then_inc(prepared, 1)
            dve.wait_ge(prep_t, 2)
            dve.wait_ge(prep_p, 2)
            n = 1
            for f in range(2):
                raw = PV[:, 4 * f:4 * f + 4].rearrange("p (m c) -> p m c", c=2)
                nc.vector.tensor_copy(w_hi[:, FC[f], :, D:DX], raw).then_inc(prep_v, 1)
                n += 1
                dve.wait_ge(prep_v, n)
                nc.vector.tensor_tensor(w_lo[:, FC[f], :, D:DX], raw,
                                        w_hi[:, FC[f], :, D:DX].bitcast(FP32), ALU.subtract).then_inc(prepared, 1)
                nc.vector.tensor_tensor(row_raw[:, FB[f], D:DX], VY[0:96, 2 * f:2 * f + 2], qkb[:, f, :],
                                        ALU.add).then_inc(prep_v, 1)
                n += 1
            nc.vector.tensor_copy(w_hi[:, WV2, :, D:DX], wg_raw).then_inc(prep_v, 1)
            n += 1
            dve.wait_ge(prep_v, n)
            nc.vector.tensor_tensor(w_lo[:, WV2, :, D:DX], wg_raw, w_hi[:, WV2, :, D:DX].bitcast(FP32),
                                    ALU.subtract).then_inc(prepared, 1)
            nc.vector.tensor_copy(row_raw[:, slot(B_SLOTS, "v2"), D:D + 1], bg).then_inc(prep_v, 1)
            n += 1
            dve.wait_ge(prep_v, n)
            src = row_raw
            for r in range(3):
                nc.vector.tensor_copy(row_part[:, :, :], src[:, :, :]).then_inc(prep_v, 1)
                n += 1
                dve.wait_ge(prep_v, n)
                nc.vector.tensor_copy(brow[32 * r:32 * r + 32, :, :],
                                      row_part[32 * r:32 * r + 32, :, :]).then_inc(prepared, 1)
                if r == 2:
                    break
                nc.vector.tensor_tensor(row_res[:, :, :], src[:, :, :], row_part[:, :, :],
                                        ALU.subtract).then_inc(prep_v, 1)
                n += 1
                dve.wait_ge(prep_v, n)
                src = row_res

        PREPARED = 2 + 5 + 3 + 1 + 2 + 1 + 3

        def matmul3(o, l_hi, l_lo, r_hi, r_lo, start, stop):
            nc.tensor.matmul(o, l_hi, r_hi, start=start, stop=False)
            nc.tensor.matmul(o, l_lo, r_hi, start=False, stop=False)
            return nc.tensor.matmul(o, l_hi, r_lo, start=False, stop=stop)

        def projected(o, t, j, w, b, cols, par):
            nc.tensor.matmul(o, ones3[:, :], brow[:, b, 0:cols], start=True, stop=False)
            for k in range(KT):
                mm = matmul3(o, xT_hi[:, par, k, j * N:(j + 1) * N], xT_lo[:, par, k, j * N:(j + 1) * N],
                             w_hi[:, w, k, 0:cols], w_lo[:, w, k, 0:cols], False, k == KT - 1)
            return mm

        def stage_x(sp, layer, staged, xt_ready):
            def one(i, par):
                wait(sp, xt_ready, i - 1)
                if layer:
                    wait(sp, xfinal[layer - 1], 2 * i + 2)
                sp.dma_start(xin[:, par, :, :].rearrange("p a d -> p (a d)"),
                             X[:, bass.ds(i * 2 * D, 2 * D)]).then_inc(staged[par], 16)
            if layer == 0:
                per = PAIRS // CHUNKS
                for c in range(CHUNKS):
                    sp.wait_ge(load_x[c], 16)
                    for i in range(c * per, (c + 1) * per):
                        one(i, i % 2)
            else:
                steps(sp, 0, PAIRS - 1, 2, PAIRS, one)

        def attention(layer):
            L = f"{layer}"
            normed = layer == 0
            wq, wk, wv = (slot(W_SLOTS, c + L) for c in "qkv")
            bv = slot(B_SLOTS, "v" + L)
            cq, ck = (0, 1) if layer == 0 else (2, 3)
            staged = [sem(f"staged{L}_{p}") for p in range(2)]
            xt_ready, xt_hi, xt_lo = sem("xt_ready" + L), sem("xt_hi" + L), sem("xt_lo" + L)
            q_ready, q_done = sem("q_ready" + L), sem("q_done" + L)
            k_ready, k_done_a, k_done_v = sem("k_ready" + L), sem("k_done_a" + L), sem("k_done_v" + L)
            v_ready, v_done = sem("v_ready" + L), sem("v_done" + L)
            s_ready, max_done = sem("s_ready" + L), sem("max_done" + L)
            exp_half, mul_half = sem("exp_half" + L), sem("mul_half" + L)
            at_ready, at_done = sem("at_ready" + L), sem("at_done" + L)
            pv_ready, rec_done, norm_done = sem("pv_ready" + L), sem("rec_done" + L), sem("norm_done" + L)
            adj_ready = sem("adj_ready" + L)
            ot_ready, ot_hi, ot_lo = sem("ot_ready" + L), sem("ot_hi" + L), sem("ot_lo" + L)
            y_ready, res_done, st_done = sem("y_ready" + L), sem("res_done" + L), sem("st_done" + L)
            mv_done, ve_done, rstd_done = sem("mv_done" + L), sem("ve_done" + L), sem("rstd_done" + L)
            z_done = sem("z_done" + L)
            log_done, kb_ready, edge_done = sem("log_done" + L), sem("kb_ready" + L), sem("edge_done" + L)
            sum_done = sem("sum_done" + L)
            VB = [VY, XO]
            final = xfinal[layer]

            def start(eng):
                if layer:
                    eng.wait_ge(xfinal[layer - 1], B)
                else:
                    eng.wait_ge(prepared, PREPARED)

            progs["sync"].append(lambda sp: (start(sp), stage_x(sp, layer, staged, xt_ready)))

            def pool_step(t, par):
                for j in range(2):
                    g = 2 * t + j
                    wait(nc.gpsimd, mv_done, g + 1)
                    nc.gpsimd.tensor_tensor(veps[:, j, :], mv[:, j, 1:2], ln_eps[:, :], ALU.add)\
                        .then_inc(ve_done, 1)
                    wait(nc.gpsimd, ve_done, g + 1)
                    wait(nc.gpsimd, final, g - 1)
                    nc.gpsimd.tensor_tensor(rstd[:, j, :], veps[:, j, :], mhalf[:, :], ALU.pow)\
                        .then_inc(rstd_done, 1)

            def pool_prog(pool):
                if normed:
                    start(pool)
                    steps(pool, 0, PAIRS - 1, 2, PAIRS, pool_step)
            progs["gpsimd"].append(pool_prog)

            def transpose_x(pe, i, par):
                pe.wait_ge(staged[par], 8 * (i - par) + 16)
                wait(pe, xt_lo, i)
                if normed:
                    wait(pe, ot_lo, i - 2)
                else:
                    wait(pe, edge_done, 2 * i)
                for k in range(KT):
                    for j in range(2):
                        mm = nc.tensor.transpose(XO[:, k * PN + j * N:k * PN + (j + 1) * N],
                                                 xin[:, par, j, k * P:(k + 1) * P], ident[:, :])
                mm.then_inc(xt_ready, 1)

            def project_t(o_bank, w, par, ready):
                for m in range(KT):
                    for k in range(KT):
                        mm = matmul3(o_bank[:, m * PN:(m + 1) * PN],
                                     w_hi[:, w, k, m * P:(m + 1) * P], w_lo[:, w, k, m * P:(m + 1) * P],
                                     xT_hi[:, par, k, :], xT_lo[:, par, k, :], k == 0, k == KT - 1)
                mm.then_inc(ready, 1)

            def scores(pe, g, j, par):
                if normed:
                    wait(pe, exp_half, 2 * g)
                else:
                    wait(pe, sum_done, g)
                for m in range(KT):
                    mm = nc.tensor.matmul(SC[:, m * HPT:(m + 1) * HPT, :].rearrange("p h n -> p (h n)"),
                                          QT[:, par, m, j * N:(j + 1) * N],
                                          KBD[:, m, j, :, :].rearrange("p h n -> p (h n)"),
                                          start=True, stop=True)
                mm.then_inc(s_ready, 1)

            def transpose_att(pe, g, j):
                wait(pe, mul_half if normed else exp_half, 2 * g + 2)
                wait(pe, at_done, g)
                for h in range(H):
                    mm = nc.tensor.transpose(AT[:, h, :], att[:, j, h, :], ident[:, :])
                mm.then_inc(at_ready, 1)

            def values(pe, g, j, par):
                wait(pe, at_done, g + 1)
                wait(pe, norm_done, g)
                for h in range(H):
                    mm = nc.tensor.matmul(PV[:, h * DV:(h + 1) * DV], attT[:, j, h, :],
                                          V[:, par, j, h, :], start=True, stop=True)
                mm.then_inc(pv_ready, 1)

            def pe_step(t, par):
                pe = nc.tensor
                a, b, bp = 2 * (t - 1), 2 * (t - 1) + 1, 2 * (t - 1) - 1
                proj = within(t, 0, PAIRS)
                here = within(t, 1, PAIRS + 1)
                last = within(t, 2, PAIRS + 2)
                if here:
                    pe.wait_ge(q_done, t)
                    pe.wait_ge(k_done_a, t)
                    pe.wait_ge(k_done_v, t)
                    scores(pe, a, 0, 1 - par)
                if proj:
                    pe.wait_ge(xt_hi, t + 1)
                    pe.wait_ge(xt_lo, t + 1)
                    project_t(QK, wq, par, q_ready)
                if last:
                    transpose_att(pe, bp, 1)
                if proj:
                    if normed:
                        wait(pe, res_done, 2 * (t - 2))
                    else:
                        wait(pe, edge_done, 2 * t)
                    wait(pe, v_done, t)
                    for j in range(2):
                        o = VY[:, j * D:(j + 1) * D] if normed else VB[j][:, 0:DX]
                        mm = projected(o, t, j, wv, bv, D if normed else DX, par)
                    mm.then_inc(v_ready, 1)
                    pe.wait_ge(q_done, t + 1)
                    project_t(QK, wk, par, k_ready)
                if last:
                    pe.wait_ge(v_done, t - 1)
                    values(pe, bp, 1, par)
                if proj and not normed:
                    pe.wait_ge(v_done, t + 1)
                    for j in range(2):
                        mm = nc.tensor.transpose(VB[j][:, 3 * N:4 * N],
                                                 node_b[:, par, j, 1:2].broadcast_to([P, P]), ident[:, :])
                    mm.then_inc(kb_ready, 1)
                if here:
                    scores(pe, b, 1, 1 - par)
                if last and normed:
                    pe.wait_ge(norm_done, 2 * (t - 1))
                    wait(pe, xt_lo, t + 1 if not isinstance(t, int) else min(t + 1, PAIRS))
                    for k in range(KT):
                        for j in range(2):
                            mm = nc.tensor.transpose(XO[:, k * PN + j * N:k * PN + (j + 1) * N],
                                                     onorm[:, j, k * P:(k + 1) * P], ident[:, :])
                    mm.then_inc(ot_ready, 1)
                if here:
                    transpose_att(pe, a, 0)
                if last and normed:
                    pe.wait_ge(ot_hi, t - 1)
                    pe.wait_ge(ot_lo, t - 1)
                    wait(pe, v_done, t + 1 if not isinstance(t, int) else min(t + 1, PAIRS))
                    for j in range(2):
                        o = VY[:, j * D:(j + 1) * D]
                        nc.tensor.matmul(o, ones3[:, :], brow[:, slot(B_SLOTS, "o0"), 0:D],
                                         start=True, stop=False)
                        for k in range(KT):
                            wo = slot(W_SLOTS, "o0")
                            mm = matmul3(o, oT_hi[:, k, j * N:(j + 1) * N], oT_lo[:, k, j * N:(j + 1) * N],
                                         w_hi[:, wo, k, 0:D], w_lo[:, wo, k, 0:D], False, k == KT - 1)
                    mm.then_inc(y_ready, 1)
                if here:
                    pe.wait_ge(v_done, t)
                    values(pe, a, 0, 1 - par)
                if within(t, -1, PAIRS - 1):
                    transpose_x(pe, t + 1, 1 - par)

            def pe_prog(pe):
                start(pe)
                transpose_x(pe, 0, 0)
                steps(pe, 0, PAIRS + 1, 4, PAIRS - 2, pe_step)
            progs["tensor"].append(pe_prog)

            def exps(act, g, j):
                act.wait_ge(max_done, g + 1)
                wait(act, at_ready, g - 1)
                src = SC[:, :, :] if normed else att[:, j, :, :]
                for h in range(H):
                    ins = nc.scalar.activation(att[:, j, h, :], src[:, h, :], ACT.Exp,
                                               bias=negmax[:, j, h:h + 1])
                    if h % HPT == HPT - 1:
                        ins.then_inc(exp_half, 1)

            def evac_att(act, g, j):
                act.wait_ge(at_ready, g + 1)
                wait(act, pv_ready, g - 1)
                nc.scalar.copy(attT[:, j, :, :], AT[:, :, :]).then_inc(at_done, 1)

            def evac_x(act, i, par):
                act.wait_ge(xt_ready, i + 1)
                wait(act, k_ready, i - 1)
                wait(act, v_ready, i - 1)
                nc.scalar.copy(xT_hi[:, par, :, :], XO[:, :].rearrange("p (k n) -> p k n", k=KT))\
                    .then_inc(xt_hi, 1)

            def act_step(t, par):
                act = nc.scalar
                a, b, bp = 2 * (t - 1), 2 * (t - 1) + 1, 2 * (t - 1) - 1
                proj = within(t, 0, PAIRS)
                here = within(t, 1, PAIRS + 1)
                last = within(t, 2, PAIRS + 2)
                if here:
                    exps(act, a, 0)
                if proj:
                    act.wait_ge(q_ready, t + 1)
                    wait(act, s_ready, 2 * (t - 1))
                    for m in range(KT):
                        ins = nc.scalar.activation(QT[:, par, m, :], QK[:, m * PN:(m + 1) * PN], ACT.Identity,
                                                   bias=bcol[:, cq, m:m + 1], scale=float(DK) ** -0.5)
                    ins.then_inc(q_done, 1)
                if last:
                    evac_att(act, bp, 1)
                if proj:
                    act.wait_ge(v_ready, t + 1)
                    wait(act, pv_ready, 2 * (t - 1))
                    if normed:
                        nc.scalar.copy(V[:, par, :, :, 0:DK],
                                       VY[:, :].rearrange("p (j h d) -> p j h d", j=2, h=H)).then_inc(v_done, 1)
                    else:
                        wait(act, edge_done, 2 * (t - 1))
                        for j in range(2):
                            nc.scalar.copy(V[:, par, j, :, 0:DK], VB[j][:, 0:D].rearrange("p (h d) -> p h d", h=H))
                            ins = nc.scalar.copy(node_b[:, par, j, :], VB[j][:, D:DX])
                        ins.then_inc(v_done, 1)
                        nc.scalar.activation(log_adj[:, par, :, :].rearrange("p j n -> p (j n)"),
                                             ADJ[:, bass.ds(t * PN, PN)], ACT.Ln, bias=eps_col[:, :])\
                            .then_inc(log_done, 1)
                if last and normed:
                    act.wait_ge(ot_ready, t - 1)
                    wait(act, y_ready, t - 2)
                    nc.scalar.copy(oT_hi[:, :, :], XO[:, :].rearrange("p (k n) -> p k n", k=KT))\
                        .then_inc(ot_hi, 1)
                if here:
                    evac_att(act, a, 0)
                if proj:
                    act.wait_ge(k_ready, t + 1)
                    wait(act, s_ready, 2 * t)
                    for m in range(KT):
                        for r in range(2):
                            q = slice(r * DK, (r + 1) * DK)
                            ins = nc.scalar.activation(
                                KBD[q, m, :, r, :], QK[q, m * PN:(m + 1) * PN].rearrange("p (j n) -> p j n", j=2),
                                ACT.Identity, bias=bcol[q, ck, m:m + 1])
                    ins.then_inc(k_done_a, 1)
                if here:
                    exps(act, b, 1)
                if within(t, -1, PAIRS - 1):
                    evac_x(act, t + 1, 1 - par)

            def act_prog(act):
                start(act)
                evac_x(act, 0, 0)
                steps(act, 0, PAIRS + 1, 4, PAIRS - 2, act_step)
            progs["scalar"].append(act_prog)

            def head_max(dve, g, j, epar):
                dve.wait_ge(s_ready, g + 1)
                wait(dve, exp_half, 2 * (g - 1))
                src = SC[:, :, :]
                if not normed:
                    dve.wait_ge(edge_done, g + 1)
                    wait(dve, at_ready, g - 1)
                    src = att[:, j, :, :]
                    nc.vector.tensor_tensor(src, SC[:, :, :],
                                            edge_b[:, epar, j, :].unsqueeze(1).broadcast_to([P, H, N]),
                                            ALU.add).then_inc(sum_done, 1)
                    dve.wait_ge(sum_done, g + 1)
                nc.vector.tensor_reduce(negmax[:, j, :], src, AX.X, ALU.max, negate=True)\
                    .then_inc(max_done, 1)

            def edge_bias(dve, t, par):
                dve.wait_ge(kb_ready, t + 1)
                dve.wait_ge(log_done, t + 1)
                wait(dve, sum_done, 2 * (t - 1))
                for j in range(2):
                    nc.vector.scalar_tensor_tensor(edge_b[:, par, j, :], VB[j][:, 3 * N:4 * N],
                                                   node_b[:, par, j, 0:1], log_adj[:, par, j, :],
                                                   ALU.add, ALU.add).then_inc(edge_done, 1)

            def clip_adj(dve, t, par):
                wait(dve, mul_half, 4 * (t - 1))
                nc.vector.tensor_scalar(adjw[:, par, :, :].rearrange("p j n -> p (j n)"),
                                        ADJ[:, bass.ds(t * PN, PN)], ADJ_MIN, None, ALU.max)\
                    .then_inc(adj_ready, 1)

            def weigh(dve, g, j, t, par):
                dve.wait_ge(adj_ready, t)
                for hf in range(2):
                    dve.wait_ge(exp_half, 2 * g + 1 + hf)
                    part = att[:, j, hf * HPT:(hf + 1) * HPT, :]
                    nc.vector.tensor_tensor(part, part,
                                            adjw[:, par, j, :].unsqueeze(1).broadcast_to([P, HPT, N]),
                                            ALU.mult).then_inc(mul_half, 1)

            def norm(dve, g, j):
                dve.wait_ge(pv_ready, g + 1)
                o = PV[:, 0:H * DV].rearrange("p (h d) -> p h d", h=H)
                nc.vector.reciprocal(rsum[:, j, :], o[:, :, DK]).then_inc(rec_done, 1)
                dve.wait_ge(rec_done, g + 1)

            def finish_norm(dve, g, j, pair):
                norm(dve, g, j)
                o = PV[:, 0:H * DV].rearrange("p (h d) -> p h d", h=H)
                if normed:
                    wait(dve, ot_ready, pair)
                else:
                    wait(dve, final, g - 1)
                nc.vector.tensor_tensor(onorm[:, j, :].rearrange("p (h d) -> p h d", h=H), o[:, :, 0:DK],
                                        rsum[:, j, :].unsqueeze(2).broadcast_to([P, H, DK]),
                                        ALU.mult).then_inc(norm_done, 1)
                if not normed:
                    dve.wait_ge(norm_done, g + 1)
                    xg = X[:, bass.ds(g * D, D)]
                    nc.vector.tensor_tensor(xg, onorm[:, j, :], xg, ALU.add).then_inc(final, 1)

            def low_x(dve, i, par):
                dve.wait_ge(xt_hi, i + 1)
                nc.vector.tensor_tensor(xT_lo[:, par, :, :], XO[:, :].rearrange("p (k n) -> p k n", k=KT),
                                        xT_hi[:, par, :, :].bitcast(FP32), ALU.subtract).then_inc(xt_lo, 1)

            def layer_norm(dve, pair):
                dve.wait_ge(y_ready, pair + 1)
                for j in range(2):
                    g = 2 * pair + j
                    wait(dve, final, g - 1)
                    nc.vector.tensor_tensor(yres[:, j, :], VY[:, j * D:(j + 1) * D],
                                            X[:, bass.ds(g * D, D)], ALU.add).then_inc(res_done, 1)
                for j in range(2):
                    g = 2 * pair + j
                    dve.wait_ge(res_done, g + 1)
                    nc.vector.bn_stats(stats[:, j, :], yres[:, j, :]).then_inc(st_done, 1)
                for j in range(2):
                    g = 2 * pair + j
                    dve.wait_ge(prepared, PREPARED)
                    dve.wait_ge(st_done, g + 1)
                    wait(dve, z_done, g - 1)
                    wait(dve, ve_done, g - 1)
                    nc.vector.bn_aggr(mv[:, j, :], stats[:, j, :]).then_inc(mv_done, 1)
                for j in range(2):
                    g = 2 * pair + j
                    dve.wait_ge(mv_done, g + 1)
                    nc.vector.scalar_tensor_tensor(yres[:, j, :], yres[:, j, :], mv[:, j, 0:1], gamma_b[:, :],
                                                   ALU.subtract, ALU.mult).then_inc(z_done, 1)
                for j in range(2):
                    g = 2 * pair + j
                    dve.wait_ge(z_done, g + 1)
                    dve.wait_ge(rstd_done, g + 1)
                    nc.vector.scalar_tensor_tensor(X[:, bass.ds(g * D, D)], yres[:, j, :], rstd[:, j, :],
                                                   beta_b[:, :], ALU.mult, ALU.add).then_inc(final, 1)

            def dve_step(t, par):
                dve = nc.vector
                a, b, bp = 2 * (t - 1), 2 * (t - 1) + 1, 2 * (t - 1) - 1
                proj = within(t, 0, PAIRS)
                here = within(t, 1, PAIRS + 1)
                last = within(t, 2, PAIRS + 2)
                if here:
                    head_max(dve, a, 0, 1 - par)
                    if normed:
                        weigh(dve, a, 0, t, 1 - par)
                if last:
                    finish_norm(dve, bp, 1, t - 2)
                if here:
                    head_max(dve, b, 1, 1 - par)
                if last and normed:
                    dve.wait_ge(ot_hi, t - 1)
                    nc.vector.tensor_tensor(oT_lo[:, :, :], XO[:, :].rearrange("p (k n) -> p k n", k=KT),
                                            oT_hi[:, :, :].bitcast(FP32), ALU.subtract).then_inc(ot_lo, 1)
                if proj:
                    dve.wait_ge(k_ready, t + 1)
                    wait(dve, s_ready, 2 * t)
                    for m in range(KT):
                        for r in range(2, HPT):
                            q = slice(r * DK, (r + 1) * DK)
                            ins = nc.vector.tensor_scalar(
                                KBD[q, m, :, r, :], QK[q, m * PN:(m + 1) * PN].rearrange("p (j n) -> p j n", j=2),
                                bcol[q, ck, m:m + 1], None, ALU.add)
                    ins.then_inc(k_done_v, 1)
                if proj and normed:
                    clip_adj(dve, t, par)
                if proj and not normed:
                    edge_bias(dve, t, par)
                if here and normed:
                    weigh(dve, b, 1, t, 1 - par)
                if last and normed:
                    layer_norm(dve, t - 2)
                if here:
                    finish_norm(dve, a, 0, t - 1)
                if within(t, -1, PAIRS - 1):
                    low_x(dve, t + 1, 1 - par)

            def dve_prog(dve):
                start(dve)
                if layer == 0:
                    for c in range(CHUNKS):
                        dve.wait_ge(load_adj[c], 16)
                low_x(dve, 0, 0)
                steps(dve, 0, PAIRS + 1, 4, PAIRS - 2, dve_step)
            progs["vector"].append(dve_prog)

        def masked_layer(layer):
            L = f"{layer}"
            w = slot(W_SLOTS, "fc" + L)
            br = slot(B_SLOTS, "fc" + L)
            staged = [sem(f"staged{L}_{p}") for p in range(2)]
            xt_ready, xt_hi, xt_lo = sem("xt_ready" + L), sem("xt_hi" + L), sem("xt_lo" + L)
            v_ready, v_done = sem("v_ready" + L), sem("v_done" + L)
            kb_ready, logit_done, leaky_done = sem("kb_ready" + L), sem("logit_done" + L), sem("leaky_done" + L)
            max_done, exp_done, mask_ready = sem("max_done" + L), sem("exp_done" + L), sem("mask_ready" + L)
            pt_ready, pt_done, pv_ready, rec_done = (sem(n + L) for n in ("pt_ready", "pt_done", "pv_ready", "rec_done"))
            final = xfinal[layer]
            VB = [QK, VY]
            KB = SC[:, 0:2, :]
            PT = AT[:, 0:2, :]

            def start(eng):
                eng.wait_ge(xfinal[layer - 1], B)

            progs["sync"].append(lambda sp: (start(sp), stage_x(sp, layer, staged, xt_ready)))

            def transpose_x(pe, i, par):
                pe.wait_ge(staged[par], 8 * (i - par) + 16)
                wait(pe, xt_lo, i)
                for k in range(KT):
                    for j in range(2):
                        mm = nc.tensor.transpose(XO[:, k * PN + j * N:k * PN + (j + 1) * N],
                                                 xin[:, par, j, k * P:(k + 1) * P], ident[:, :])
                mm.then_inc(xt_ready, 1)

            def pe_step(t, par):
                pe = nc.tensor
                proj = within(t, 0, PAIRS)
                last = within(t, 1, PAIRS + 1)
                if proj:
                    pe.wait_ge(xt_hi, t + 1)
                    pe.wait_ge(xt_lo, t + 1)
                    wait(pe, v_done, t)
                    for j in range(2):
                        mm = projected(VB[j][:, 0:DX], t, j, w, br, DX, par)
                    mm.then_inc(v_ready, 1)
                if last:
                    pe.wait_ge(exp_done, 2 * t)
                    wait(pe, pt_done, t - 1)
                    for j in range(2):
                        mm = nc.tensor.transpose(PT[:, j, :], prob[:, j, :], ident[:, :])
                    mm.then_inc(pt_ready, 1)
                if within(t, 0, PAIRS - 1):
                    transpose_x(pe, t + 1, 1 - par)
                if proj:
                    pe.wait_ge(v_done, t + 1)
                    wait(pe, logit_done, 2 * t)
                    for j in range(2):
                        mm = nc.tensor.transpose(KB[:, j, :], VX[:, par, j, D + 1:D + 2].broadcast_to([P, P]),
                                                 ident[:, :])
                    mm.then_inc(kb_ready, 1)
                if last:
                    pe.wait_ge(pt_done, t)
                    wait(pe, final, 2 * (t - 1))
                    for j in range(2):
                        mm = nc.tensor.matmul(PV[:, j * D:(j + 1) * D], probT[:, j, :],
                                              VX[:, 1 - par, j, 0:D], start=True, stop=True)
                    mm.then_inc(pv_ready, 1)

            def pe_prog(pe):
                start(pe)
                transpose_x(pe, 0, 0)
                steps(pe, 0, PAIRS, 2, PAIRS - 2, pe_step)
            progs["tensor"].append(pe_prog)

            def evac_x(act, i, par):
                act.wait_ge(xt_ready, i + 1)
                wait(act, v_ready, i - 1)
                nc.scalar.copy(xT_hi[:, par, :, :], XO[:, :].rearrange("p (k n) -> p k n", k=KT))\
                    .then_inc(xt_hi, 1)

            def act_step(t, par):
                act = nc.scalar
                if within(t, 0, PAIRS):
                    act.wait_ge(v_ready, t + 1)
                    wait(act, pv_ready, t - 1)
                    for j in range(2):
                        ins = nc.scalar.copy(VX[:, par, j, :], VB[j][:, 0:DX])
                    ins.then_inc(v_done, 1)
                if within(t, 1, PAIRS + 1):
                    act.wait_ge(pt_ready, t)
                    wait(act, pv_ready, t - 1)
                    nc.scalar.copy(probT[:, :, :], PT).then_inc(pt_done, 1)
                if within(t, 0, PAIRS - 1):
                    evac_x(act, t + 1, 1 - par)
                if within(t, 0, PAIRS):
                    act.wait_ge(max_done, t + 1)
                    wait(act, pt_ready, t)
                    wait(act, rec_done, t)
                    for j in range(2):
                        nc.scalar.activation(prob[:, j, :], leaky[:, j, :], ACT.Exp, bias=nmax1[:, j:j + 1],
                                             accum_out=psum1[:, j:j + 1]).then_inc(exp_done, 1)

            def act_prog(act):
                start(act)
                evac_x(act, 0, 0)
                steps(act, 0, PAIRS, 2, PAIRS - 2, act_step)
            progs["scalar"].append(act_prog)

            def low_x(dve, i, par):
                dve.wait_ge(xt_hi, i + 1)
                nc.vector.tensor_tensor(xT_lo[:, par, :, :], XO[:, :].rearrange("p (k n) -> p k n", k=KT),
                                        xT_hi[:, par, :, :].bitcast(FP32), ALU.subtract).then_inc(xt_lo, 1)

            def dve_step(t, par):
                dve = nc.vector
                if within(t, 0, PAIRS - 1):
                    low_x(dve, t + 1, 1 - par)
                if within(t, 0, PAIRS):
                    wait(dve, logit_done, 2 * t)
                    nc.vector.tensor_scalar(mbias[:, :, :].rearrange("p j n -> p (j n)"),
                                            ADJ[:, bass.ds(t * PN, PN)], -1.0, MASKED, ALU.add, ALU.mult)\
                        .then_inc(mask_ready, 1)
                    dve.wait_ge(kb_ready, t + 1)
                    dve.wait_ge(mask_ready, t + 1)
                    wait(dve, leaky_done, t)
                    for j in range(2):
                        nc.vector.scalar_tensor_tensor(logit[:, j, :], KB[:, j, :], VX[:, par, j, D:D + 1],
                                                       mbias[:, j, :], ALU.add, ALU.add)\
                            .then_inc(logit_done, 1)
                    dve.wait_ge(logit_done, 2 * t + 2)
                    wait(dve, exp_done, 2 * t)
                    nc.vector.scalar_tensor_tensor(leaky[:, :, :], logit[:, :, :], LEAKY, logit[:, :, :],
                                                   ALU.mult, ALU.max).then_inc(leaky_done, 1)
                    dve.wait_ge(leaky_done, t + 1)
                    nc.vector.tensor_reduce(nmax1[:, :], leaky[:, :, :], AX.X, ALU.max, negate=True)\
                        .then_inc(max_done, 1)
                if within(t, 1, PAIRS + 1):
                    dve.wait_ge(pv_ready, t)
                    dve.wait_ge(rec_done, t)
                    for j in range(2):
                        xg = X[:, bass.ds((2 * (t - 1) + j) * D, D)]
                        nc.vector.scalar_tensor_tensor(xg, PV[:, j * D:(j + 1) * D], prec[:, j:j + 1], xg,
                                                       ALU.mult, ALU.add).then_inc(final, 1)
                if within(t, 0, PAIRS):
                    dve.wait_ge(exp_done, 2 * t + 2)
                    wait(dve, final, 2 * t)
                    nc.vector.reciprocal(prec[:, :], psum1[:, :]).then_inc(rec_done, 1)

            def dve_prog(dve):
                start(dve)
                low_x(dve, 0, 0)
                steps(dve, 0, PAIRS, 2, PAIRS - 2, dve_step)
            progs["vector"].append(dve_prog)

        def stores(sp):
            with sp.Fori(0, PAIRS) as i:
                sp.wait_ge(xfinal[3], 2 * i + 2)
                sp.dma_start(out[bass.ds(i * 2, 2)].rearrange("g p d -> p g d"),
                             X[:, bass.ds(i * 2 * D, 2 * D)].rearrange("p (g d) -> p g d", g=2))\
                    .then_inc(stored, 16)
            sp.wait_ge(stored, 16 * PAIRS)

        progs["sync"].append(sync_prep)
        progs["scalar"].append(scalar_prep)
        progs["gpsimd"].append(gpsimd_prep)
        progs["tensor"].append(tensor_prep)
        progs["vector"].append(vector_prep)
        attention(0)
        masked_layer(1)
        attention(2)
        masked_layer(3)
        progs["sync"].append(stores)

        @block.sync
        def _(sp):
            for part in progs["sync"]:
                part(sp)

        @block.gpsimd
        def _(pool):
            for part in progs["gpsimd"]:
                part(pool)

        @block.scalar
        def _(act):
            for part in progs["scalar"]:
                part(act)

        @block.tensor
        def _(pe):
            for part in progs["tensor"]:
                part(pe)

        @block.vector
        def _(dve):
            for part in progs["vector"]:
                part(dve)


def kernel(**inputs):
    import numpy as np
    import concourse.bacc as bacc
    from concourse.bass_utils import run_bass_kernel_spmd

    a = {k: np.asarray(v) for k, v in inputs.items()}

    def tiles(w):
        return w.reshape(2, 128, -1).transpose(1, 0, 2)

    fwd = [a["L0_gnn_Wq"].T, a["L0_gnn_Wk"].T, a["L0_gnn_Wv"].T, a["L0_gnn_Wo"].T, a["L1_gnn_fc_w"].T,
           a["L2_gnn_W_q"], a["L2_gnn_W_k"], a["L2_gnn_W_v"], a["L3_gnn_W_fc"]]
    rev = [a["L1_gnn_fc_w"], a["L3_gnn_W_fc"].T]
    qkw = [np.stack([a["L1_gnn_q_w"][0], a["L1_gnn_k_w"][0]], 1),
           np.concatenate([a["L3_gnn_w_q"], a["L3_gnn_w_k"]], 1)]
    cols = [a[n] for n in ("L0_gnn_bq", "L0_gnn_bk", "L2_gnn_b_q", "L2_gnn_b_k", "L1_gnn_fc_b", "L3_gnn_b_fc")]
    rows = [a[n] for n in ("L0_gnn_bv", "L0_gnn_bo", "L1_gnn_fc_b", "L2_gnn_b_v", "L3_gnn_b_fc")]
    arrays = {
        "x": a["x"], "adj": a["adj"],
        "weights": np.stack([tiles(w) for w in fwd], 1),
        "fc_rev": np.stack([tiles(w) for w in rev], 1),
        "qk_w": np.stack([tiles(w) for w in qkw], 1),
        "bias_cols": np.stack([tiles(c)[:, :, 0] for c in cols], 1),
        "bias_rows": np.stack(rows, 0),
        "qk_b": np.stack([np.concatenate([a["L1_gnn_q_b"], a["L1_gnn_k_b"]]),
                          np.concatenate([a["L3_gnn_b_q"], a["L3_gnn_b_k"]])], 0),
        "gamma": a["L0_gnn_gamma"], "beta": a["L0_gnn_beta"],
        "w_g": tiles(a["L2_gnn_w_g"].reshape(2, D).T), "b_g": a["L2_gnn_b_g"].reshape(1),
        "eye": np.eye(128, dtype=np.float32),
    }
    nc = bacc.Bacc("TRN2", target_bir_lowering=False, num_devices=1)
    arrays = {"in_" + k: np.ascontiguousarray(v) for k, v in arrays.items()}
    args = [nc.dram_tensor(k, v.shape, mybir.dt.from_np(v.dtype), kind="ExternalInput").ap()
            for k, v in arrays.items()]
    out = nc.dram_tensor("out", [B, N, D], FP32, kind="ExternalOutput").ap()
    build(nc, *args, out)
    r = run_bass_kernel_spmd(nc, [arrays], core_ids=[0])
    return r.results[0]["out"]
```

```python
from contextlib import ExitStack

import concourse.bass as bass
from concourse import mybir

FP32 = mybir.dt.float32
FP32R = mybir.dt.float32r
BF16 = mybir.dt.bfloat16
ALU = mybir.AluOpType
ACT = mybir.ActivationFunctionType
AX = mybir.AxisListType

B, N, D, H = 64, 128, 256, 8
DK = D // H
P = 128
KT = D // P
HPT = P // DK
PAIRS = B // 2
PN = 2 * N
DV = DK + 1
DX = D + 2
LATE = 4
CHUNKS = 8
LN_EPS = 1e-05
ADJ_MIN = 1e-08
ADJ_EPS = 1e-09
MASKED = 1e9
LEAKY = 0.01
W_SLOTS = ["q0", "k0", "v0", "o0", "fc1", "q2", "k2", "v2", "fc3"]
B_SLOTS = ["v0", "o0", "fc1", "v2", "fc3"]


def wait(eng, sem, value):
    if isinstance(value, int) and value <= 0:
        return
    eng.wait_ge(sem, value)


def steps(eng, first, last, even_first, even_end, emit):
    for t in range(first, even_first):
        emit(t, t % 2)
    with eng.Fori(even_first, even_end - 1, 2) as t:
        emit(t, 0)
        emit(t + 1, 1)
    for t in range(even_end, last + 1):
        emit(t, t % 2)


def within(t, lo, hi):
    return not isinstance(t, int) or lo <= t < hi


def build(nc, x, adj, weights, fc_rev, qk_w, bias_cols, bias_rows, qk_b, gamma, beta, w_g, b_g, eye, out):
    ctx = ExitStack()
    with ctx:
        def sb(name, shape, dt=FP32):
            return ctx.enter_context(nc.sbuf_tensor(name, shape, dt))

        def sem(name):
            return ctx.enter_context(nc.semaphore(name))

        X = sb("X", [P, B * D])
        ADJ = sb("ADJ", [P, B * N])
        w_hi = sb("w_hi", [P, len(W_SLOTS), KT, DX], FP32R)
        w_lo = sb("w_lo", [P, len(W_SLOTS), KT, DX], FP32R)
        ident = sb("ident", [P, P])
        bcol = sb("bcol", [P, 4, KT])
        brow = sb("brow", [96, len(B_SLOTS), DX], BF16)
        ones3 = sb("ones3", [96, P], BF16)
        gamma_b = sb("gamma_b", [P, D])
        beta_b = sb("beta_b", [P, D])
        xin = sb("xin", [P, 2, 2, D])
        xT_hi = sb("xT_hi", [P, 2, KT, PN], FP32R)
        xT_lo = sb("xT_lo", [P, 2, KT, PN], FP32R)
        QT = sb("QT", [P, 2, KT, PN])
        KBD = sb("KBD", [P, 2, KT, 2, HPT, N])
        V = sb("V", [P, 2, 2, H, DV])
        negmax = sb("negmax", [P, 2, H])
        adjw = sb("adjw", [P, 2, 2, N])
        node_b = sb("node_b", [P, 2, 2, 2])
        log_adj = sb("log_adj", [P, 2, 2, N])
        edge_b = sb("edge_b", [P, 2, 2, N])
        att = sb("att", [P, 2, H, N])
        attT = sb("attT", [P, 2, H, N])
        rsum = sb("rsum", [P, 2, H])
        onorm = sb("onorm", [P, 2, D])
        oT_hi = sb("oT_hi", [P, KT, PN], FP32R)
        oT_lo = sb("oT_lo", [P, KT, PN], FP32R)
        yres = sb("yres", [P, 2, D])
        stats = sb("stats", [P, 2, 6])
        mv = sb("mv", [P, 2, 2])
        veps = sb("veps", [P, 2, 1])
        rstd = sb("rstd", [P, 2, 1])
        mhalf = sb("mhalf", [P, 1])
        eps_col = sb("eps_col", [P, 1])
        ln_eps = sb("ln_eps", [P, 1])
        spare = att[:, :, :, :].rearrange("p a h n -> p (a h n)")
        VX = spare[:, 0:4 * DX].rearrange("p (a j d) -> p a j d", a=2, j=2)
        mbias, logit, leaky = (spare[:, 4 * DX + n * PN:4 * DX + (n + 1) * PN].rearrange("p (j n) -> p j n", j=2)
                               for n in range(3))
        prob, probT = attT[:, 0, 0:2, :], attT[:, 0, 2:4, :]
        nmax1 = sb("nmax1", [P, 2])
        psum1 = sb("psum1", [P, 2])
        prec = sb("prec", [P, 2, 2])

        bank = [ctx.enter_context(nc.psum_tensor(f"bank{n}", [P, 512], FP32)) for n in range(4)]
        SC = ctx.enter_context(nc.psum_tensor("SC", [P, H, N], FP32))
        AT = ctx.enter_context(nc.psum_tensor("AT", [P, H, N], FP32))
        XO, QK, VY, PV = bank

        load_x = [sem(f"load_x{c}") for c in range(CHUNKS)]
        load_adj = [sem(f"load_adj{c}") for c in range(CHUNKS)]
        load_w = sem("load_w")
        load_c = sem("load_c")
        prep_p = sem("prep_p")
        prep_v = sem("prep_v")
        prep_t = sem("prep_t")
        prepared = sem("prepared")
        stored = sem("stored")
        xfinal = [sem(f"xfinal{l}") for l in range(4)]

        G = B // CHUNKS
        Xg = X[:, :].rearrange("p (g d) -> p g d", d=D)
        Ag = ADJ[:, :].rearrange("p (g n) -> p g n", n=N)

        free_at = [LATE * G * D]

        def early(rows, *shape):
            n = 1
            for s in shape:
                n *= s
            at = free_at[0]
            free_at[0] = at + n
            letters = "abcd"[:len(shape)]
            return X[0:rows, at:at + n].rearrange(f"p ({' '.join(letters)}) -> p {' '.join(letters)}",
                                                  **dict(zip(letters, shape)))

        w_raw = early(P, len(W_SLOTS), KT, D)
        wg_raw = early(P, KT, 2)
        qkw = early(P, 2, KT, 2)
        bfc = early(P, 2, KT)
        qkb = early(96, 2, 2)
        bg = early(96, 1)
        row_raw = early(96, len(B_SLOTS), DX)
        row_res = early(96, len(B_SLOTS), DX)
        fc_raw = att[:, :, :, :].rearrange("p a h n -> p (a h n)")[:, 0:2 * KT * D]\
            .rearrange("p (f t d) -> p f t d", f=2, t=KT)
        row_part = sb("row_part", [96, len(B_SLOTS), DX], BF16)

        def slot(names, name):
            return names.index(name)

        FC = [slot(W_SLOTS, "fc1"), slot(W_SLOTS, "fc3")]
        WV2 = slot(W_SLOTS, "v2")
        FB = [slot(B_SLOTS, "fc1"), slot(B_SLOTS, "fc3")]

        block = ctx.enter_context(nc.Block())
        progs = {"sync": [], "gpsimd": [], "scalar": [], "tensor": [], "vector": []}

        def sync_prep(sp):
            sp.dma_start(w_raw, weights).then_inc(load_w, 16)
            sp.wait_ge(load_w, 16)
            sp.wait_ge(load_c, 11 * 16)
            for c in range(CHUNKS):
                if c < LATE:
                    sp.dma_start(Xg[:, G * c:G * (c + 1), :],
                                 x[G * c:G * (c + 1)].rearrange("g p d -> p g d")).then_inc(load_x[c], 16)
                sp.dma_start(Ag[:, G * c:G * (c + 1), :],
                             adj[G * c:G * (c + 1)].rearrange("g p n -> p g n")).then_inc(load_adj[c], 16)

        def scalar_prep(act):
            act.dma_start(ident[:, :], eye).then_inc(load_c, 16)
            act.dma_start(fc_raw, fc_rev).then_inc(load_c, 16)
            act.dma_start(qkw, qk_w).then_inc(load_c, 16)
            act.dma_start(bcol[:, :, :], bias_cols[:, 0:4, :]).then_inc(load_c, 16)
            act.dma_start(bfc, bias_cols[:, 4:6, :]).then_inc(load_c, 16)
            act.dma_start(row_raw[:, :, 0:D], bias_rows.partition_broadcast(96)).then_inc(load_c, 16)
            act.dma_start(qkb, qk_b.partition_broadcast(96)).then_inc(load_c, 16)
            act.dma_start(gamma_b[:, :], gamma.partition_broadcast(P)).then_inc(load_c, 16)
            act.dma_start(beta_b[:, :], beta.partition_broadcast(P)).then_inc(load_c, 16)
            act.dma_start(wg_raw, w_g).then_inc(load_c, 16)
            act.dma_start(bg, b_g.partition_broadcast(96)).then_inc(load_c, 16)
            nc.scalar.preload_act_table_set("natural_log_exp_and_others")
            act.wait_ge(load_c, 11 * 16)
            for s in (0, 2):
                nc.scalar.mul(bcol[:, s, :], bcol[:, s, :], float(DK) ** -0.5).then_inc(prepared, 1)
            act.wait_ge(prepared, PREPARED)
            for c in range(LATE, CHUNKS):
                act.dma_start(Xg[:, G * c:G * (c + 1), :],
                              x[G * c:G * (c + 1)].rearrange("g p d -> p g d")).then_inc(load_x[c], 16)

        def gpsimd_prep(pool):
            nc.gpsimd.memset(KBD[:, :, :, :, :, :], 0.0).then_inc(prepared, 1)
            nc.gpsimd.memset(V[:, :, :, :, DK:DV], 1.0).then_inc(prepared, 1)
            nc.gpsimd.memset(mhalf[:, :], -0.5).then_inc(prepared, 1)
            nc.gpsimd.memset(eps_col[:, :], ADJ_EPS).then_inc(prepared, 1)
            nc.gpsimd.memset(ln_eps[:, :], LN_EPS).then_inc(prepared, 1)
            nc.gpsimd.memset(row_raw[:, :, D:DX], 0.0).then_inc(prep_p, 1)
            nc.gpsimd.memset(ones3[:, :], 0.0).then_inc(prep_p, 1)
            pool.wait_ge(prep_p, 2)
            for r in (0, 32, 64):
                nc.gpsimd.memset(ones3[r:r + 1, :], 1.0).then_inc(prepared, 1)

        def tensor_prep(pe):
            pe.wait_ge(load_c, 11 * 16)
            for f in range(2):
                for m in range(KT):
                    for t in range(KT):
                        mm = nc.tensor.matmul(PV[:, 4 * f + 2 * m:4 * f + 2 * m + 2],
                                              fc_raw[:, f, t, m * P:(m + 1) * P], qkw[:, f, t, :],
                                              start=(t == 0), stop=(t == KT - 1))
            mm.then_inc(prep_t, 1)
            for f in range(2):
                for t in range(KT):
                    mm = nc.tensor.matmul(VY[0:96, 2 * f:2 * f + 2],
                                          bfc[:, f, t:t + 1].broadcast_to([P, 96]), qkw[:, f, t, :],
                                          start=(t == 0), stop=(t == KT - 1))
            mm.then_inc(prep_t, 1)

        def vector_prep(dve):
            dve.wait_ge(load_w, 16)
            nc.vector.tensor_copy(w_hi[:, :, :, 0:D], w_raw).then_inc(prep_v, 1)
            dve.wait_ge(prep_v, 1)
            nc.vector.tensor_tensor(w_lo[:, :, :, 0:D], w_raw,
                                    w_hi[:, :, :, 0:D].bitcast(FP32), ALU.subtract).then_inc(prepared, 1)
            dve.wait_ge(prep_t, 2)
            dve.wait_ge(prep_p, 2)
            n = 1
            for f in range(2):
                raw = PV[:, 4 * f:4 * f + 4].rearrange("p (m c) -> p m c", c=2)
                nc.vector.tensor_copy(w_hi[:, FC[f], :, D:DX], raw).then_inc(prep_v, 1)
                n += 1
                dve.wait_ge(prep_v, n)
                nc.vector.tensor_tensor(w_lo[:, FC[f], :, D:DX], raw,
                                        w_hi[:, FC[f], :, D:DX].bitcast(FP32), ALU.subtract).then_inc(prepared, 1)
                nc.vector.tensor_tensor(row_raw[:, FB[f], D:DX], VY[0:96, 2 * f:2 * f + 2], qkb[:, f, :],
                                        ALU.add).then_inc(prep_v, 1)
                n += 1
            nc.vector.tensor_copy(w_hi[:, WV2, :, D:DX], wg_raw).then_inc(prep_v, 1)
            n += 1
            dve.wait_ge(prep_v, n)
            nc.vector.tensor_tensor(w_lo[:, WV2, :, D:DX], wg_raw, w_hi[:, WV2, :, D:DX].bitcast(FP32),
                                    ALU.subtract).then_inc(prepared, 1)
            nc.vector.tensor_copy(row_raw[:, slot(B_SLOTS, "v2"), D:D + 1], bg).then_inc(prep_v, 1)
            n += 1
            dve.wait_ge(prep_v, n)
            src = row_raw
            for r in range(3):
                nc.vector.tensor_copy(row_part[:, :, :], src[:, :, :]).then_inc(prep_v, 1)
                n += 1
                dve.wait_ge(prep_v, n)
                nc.vector.tensor_copy(brow[32 * r:32 * r + 32, :, :],
                                      row_part[32 * r:32 * r + 32, :, :]).then_inc(prepared, 1)
                if r == 2:
                    break
                nc.vector.tensor_tensor(row_res[:, :, :], src[:, :, :], row_part[:, :, :],
                                        ALU.subtract).then_inc(prep_v, 1)
                n += 1
                dve.wait_ge(prep_v, n)
                src = row_res

        PREPARED = 2 + 5 + 3 + 1 + 2 + 1 + 3

        def matmul3(o, l_hi, l_lo, r_hi, r_lo, start, stop):
            nc.tensor.matmul(o, l_hi, r_hi, start=start, stop=False)
            nc.tensor.matmul(o, l_lo, r_hi, start=False, stop=False)
            return nc.tensor.matmul(o, l_hi, r_lo, start=False, stop=stop)

        def projected(o, t, j, w, b, cols, par):
            nc.tensor.matmul(o, ones3[:, :], brow[:, b, 0:cols], start=True, stop=False)
            for k in range(KT):
                mm = matmul3(o, xT_hi[:, par, k, j * N:(j + 1) * N], xT_lo[:, par, k, j * N:(j + 1) * N],
                             w_hi[:, w, k, 0:cols], w_lo[:, w, k, 0:cols], False, k == KT - 1)
            return mm

        def stage_x(sp, layer, staged, xt_ready):
            def one(i, par):
                wait(sp, xt_ready, i - 1)
                if layer:
                    wait(sp, xfinal[layer - 1], 2 * i + 2)
                sp.dma_start(xin[:, par, :, :].rearrange("p a d -> p (a d)"),
                             X[:, bass.ds(i * 2 * D, 2 * D)]).then_inc(staged[par], 16)
            if layer == 0:
                per = PAIRS // CHUNKS
                for c in range(CHUNKS):
                    sp.wait_ge(load_x[c], 16)
                    for i in range(c * per, (c + 1) * per):
                        one(i, i % 2)
            else:
                steps(sp, 0, PAIRS - 1, 2, PAIRS, one)

        def attention(layer):
            L = f"{layer}"
            normed = layer == 0
            wq, wk, wv = (slot(W_SLOTS, c + L) for c in "qkv")
            bv = slot(B_SLOTS, "v" + L)
            cq, ck = (0, 1) if layer == 0 else (2, 3)
            staged = [sem(f"staged{L}_{p}") for p in range(2)]
            xt_ready, xt_hi, xt_lo = sem("xt_ready" + L), sem("xt_hi" + L), sem("xt_lo" + L)
            q_ready, q_done = sem("q_ready" + L), sem("q_done" + L)
            k_ready, k_done_a, k_done_v = sem("k_ready" + L), sem("k_done_a" + L), sem("k_done_v" + L)
            v_ready, v_done = sem("v_ready" + L), sem("v_done" + L)
            s_ready, max_done = sem("s_ready" + L), sem("max_done" + L)
            exp_half, mul_half = sem("exp_half" + L), sem("mul_half" + L)
            at_ready, at_done = sem("at_ready" + L), sem("at_done" + L)
            pv_ready, rec_done, norm_done = sem("pv_ready" + L), sem("rec_done" + L), sem("norm_done" + L)
            adj_ready = sem("adj_ready" + L)
            ot_ready, ot_hi, ot_lo = sem("ot_ready" + L), sem("ot_hi" + L), sem("ot_lo" + L)
            y_ready, res_done, st_done = sem("y_ready" + L), sem("res_done" + L), sem("st_done" + L)
            mv_done, ve_done, rstd_done = sem("mv_done" + L), sem("ve_done" + L), sem("rstd_done" + L)
            z_done = sem("z_done" + L)
            log_done, kb_ready, edge_done = sem("log_done" + L), sem("kb_ready" + L), sem("edge_done" + L)
            sum_done = sem("sum_done" + L)
            VB = [VY, XO]
            final = xfinal[layer]

            def start(eng):
                if layer:
                    eng.wait_ge(xfinal[layer - 1], B)
                else:
                    eng.wait_ge(prepared, PREPARED)

            progs["sync"].append(lambda sp: (start(sp), stage_x(sp, layer, staged, xt_ready)))

            def pool_step(t, par):
                for j in range(2):
                    g = 2 * t + j
                    wait(nc.gpsimd, mv_done, g + 1)
                    nc.gpsimd.tensor_tensor(veps[:, j, :], mv[:, j, 1:2], ln_eps[:, :], ALU.add)\
                        .then_inc(ve_done, 1)
                    wait(nc.gpsimd, ve_done, g + 1)
                    wait(nc.gpsimd, final, g - 1)
                    nc.gpsimd.tensor_tensor(rstd[:, j, :], veps[:, j, :], mhalf[:, :], ALU.pow)\
                        .then_inc(rstd_done, 1)

            def pool_prog(pool):
                if normed:
                    start(pool)
                    steps(pool, 0, PAIRS - 1, 2, PAIRS, pool_step)
            progs["gpsimd"].append(pool_prog)

            def transpose_x(pe, i, par):
                pe.wait_ge(staged[par], 8 * (i - par) + 16)
                wait(pe, xt_lo, i)
                if normed:
                    wait(pe, ot_lo, i - 3)
                else:
                    wait(pe, edge_done, 2 * i)
                for k in range(KT):
                    for j in range(2):
                        mm = nc.tensor.transpose(XO[:, k * PN + j * N:k * PN + (j + 1) * N],
                                                 xin[:, par, j, k * P:(k + 1) * P], ident[:, :])
                mm.then_inc(xt_ready, 1)

            def transpose_out(pe, pair):
                pe.wait_ge(norm_done, 2 * (pair + 1))
                wait(pe, xt_lo, pair + 4 if not isinstance(pair, int) else min(pair + 4, PAIRS))
                for k in range(KT):
                    for j in range(2):
                        mm = nc.tensor.transpose(XO[:, k * PN + j * N:k * PN + (j + 1) * N],
                                                 onorm[:, j, k * P:(k + 1) * P], ident[:, :])
                mm.then_inc(ot_ready, 1)

            def project_out(pe, pair):
                pe.wait_ge(ot_hi, pair + 1)
                pe.wait_ge(ot_lo, pair + 1)
                wait(pe, v_done, pair + 3 if not isinstance(pair, int) else min(pair + 3, PAIRS))
                wo = slot(W_SLOTS, "o0")
                for j in range(2):
                    o = VY[:, j * D:(j + 1) * D]
                    nc.tensor.matmul(o, ones3[:, :], brow[:, slot(B_SLOTS, "o0"), 0:D], start=True, stop=False)
                    for k in range(KT):
                        mm = matmul3(o, oT_hi[:, k, j * N:(j + 1) * N], oT_lo[:, k, j * N:(j + 1) * N],
                                     w_hi[:, wo, k, 0:D], w_lo[:, wo, k, 0:D], False, k == KT - 1)
                mm.then_inc(y_ready, 1)

            def project_v(pe, t, par):
                if normed:
                    wait(pe, res_done, 2 * (t - 2))
                else:
                    wait(pe, xt_lo, t + 1)
                    wait(pe, edge_done, 2 * t)
                wait(pe, v_done, t)
                for j in range(2):
                    o = VY[:, j * D:(j + 1) * D] if normed else VB[j][:, 0:DX]
                    mm = projected(o, t, j, wv, bv, D if normed else DX, par)
                mm.then_inc(v_ready, 1)

            def spread_keys(pe, t, par):
                pe.wait_ge(v_done, t + 1)
                for j in range(2):
                    mm = nc.tensor.transpose(VB[j][:, 3 * N:4 * N],
                                             node_b[:, par, j, 1:2].broadcast_to([P, P]), ident[:, :])
                mm.then_inc(kb_ready, 1)

            def project_t(o_bank, w, par, ready):
                for m in range(KT):
                    for k in range(KT):
                        mm = matmul3(o_bank[:, m * PN:(m + 1) * PN],
                                     w_hi[:, w, k, m * P:(m + 1) * P], w_lo[:, w, k, m * P:(m + 1) * P],
                                     xT_hi[:, par, k, :], xT_lo[:, par, k, :], k == 0, k == KT - 1)
                mm.then_inc(ready, 1)

            def scores(pe, g, j, par):
                if normed:
                    wait(pe, exp_half, 2 * g)
                else:
                    wait(pe, sum_done, g)
                for m in range(KT):
                    mm = nc.tensor.matmul(SC[:, m * HPT:(m + 1) * HPT, :].rearrange("p h n -> p (h n)"),
                                          QT[:, par, m, j * N:(j + 1) * N],
                                          KBD[:, par, m, j, :, :].rearrange("p h n -> p (h n)"),
                                          start=True, stop=True)
                mm.then_inc(s_ready, 1)

            def transpose_att(pe, g, j):
                wait(pe, mul_half if normed else exp_half, 2 * g + 2)
                wait(pe, at_done, g)
                for h in range(H):
                    mm = nc.tensor.transpose(AT[:, h, :], att[:, j, h, :], ident[:, :])
                mm.then_inc(at_ready, 1)

            def values(pe, g, j, par):
                wait(pe, at_done, g + 1)
                wait(pe, norm_done, g)
                for h in range(H):
                    mm = nc.tensor.matmul(PV[:, h * DV:(h + 1) * DV], attT[:, j, h, :],
                                          V[:, par, j, h, :], start=True, stop=True)
                mm.then_inc(pv_ready, 1)

            def pe_step(t, par):
                pe = nc.tensor
                a, b, bp = 2 * (t - 1), 2 * (t - 1) + 1, 2 * (t - 1) - 1
                proj = within(t, 0, PAIRS)
                here = within(t, 1, PAIRS + 1)
                last = within(t, 2, PAIRS + 2)
                more = within(t, -1, PAIRS - 1)
                if here:
                    pe.wait_ge(q_done, t)
                    pe.wait_ge(k_done_a, t)
                    pe.wait_ge(k_done_v, t)
                    scores(pe, a, 0, 1 - par)
                if proj:
                    pe.wait_ge(xt_hi, t + 1)
                    pe.wait_ge(xt_lo, t + 1)
                    wait(pe, k_done_a, t)
                    wait(pe, k_done_v, t)
                    project_t(QK, wq, par, q_ready)
                if last:
                    transpose_att(pe, bp, 1)
                if normed and more:
                    transpose_x(pe, t + 1, 1 - par)
                if proj:
                    project_v(pe, t, par)
                    if not normed:
                        pe.wait_ge(q_done, t + 1)
                        project_t(QK, wk, par, k_ready)
                if last:
                    pe.wait_ge(v_done, t - 1)
                    values(pe, bp, 1, par)
                if here:
                    scores(pe, b, 1, 1 - par)
                if normed and last:
                    transpose_out(pe, t - 2)
                if proj:
                    if normed:
                        pe.wait_ge(q_done, t + 1)
                        project_t(QK, wk, par, k_ready)
                    else:
                        spread_keys(pe, t, par)
                if here:
                    transpose_att(pe, a, 0)
                if not normed and more:
                    transpose_x(pe, t + 1, 1 - par)
                if normed and last:
                    project_out(pe, t - 2)
                if here:
                    pe.wait_ge(v_done, t)
                    values(pe, a, 0, 1 - par)

            def pe_prog(pe):
                start(pe)
                transpose_x(pe, 0, 0)
                steps(pe, 0, PAIRS + 1, 4, PAIRS - 2, pe_step)
            progs["tensor"].append(pe_prog)

            def exps(act, g, j, hf):
                if hf == 0:
                    act.wait_ge(max_done, g + 1)
                    wait(act, at_ready, g - 1)
                src = SC[:, :, :] if normed else att[:, j, :, :]
                for h in range(hf * HPT, (hf + 1) * HPT):
                    ins = nc.scalar.activation(att[:, j, h, :], src[:, h, :], ACT.Exp,
                                               bias=negmax[:, j, h:h + 1])
                ins.then_inc(exp_half, 1)

            def evac_att(act, g, j):
                act.wait_ge(at_ready, g + 1)
                wait(act, pv_ready, g - 1)
                nc.scalar.copy(attT[:, j, :, :], AT[:, :, :]).then_inc(at_done, 1)

            def evac_x(act, i, par):
                act.wait_ge(xt_ready, i + 1)
                wait(act, k_ready, i - 1)
                wait(act, v_ready, i - 1)
                nc.scalar.copy(xT_hi[:, par, :, :], XO[:, :].rearrange("p (k n) -> p k n", k=KT))\
                    .then_inc(xt_hi, 1)

            def evac_q(act, t, par):
                act.wait_ge(q_ready, t + 1)
                wait(act, s_ready, 2 * (t - 1))
                for m in range(KT):
                    ins = nc.scalar.activation(QT[:, par, m, :], QK[:, m * PN:(m + 1) * PN], ACT.Identity,
                                               bias=bcol[:, cq, m:m + 1], scale=float(DK) ** -0.5)
                ins.then_inc(q_done, 1)

            def evac_k(act, t, par):
                act.wait_ge(k_ready, t + 1)
                wait(act, s_ready, 2 * (t - 1))
                for m in range(KT):
                    for r in range(2):
                        q = slice(r * DK, (r + 1) * DK)
                        ins = nc.scalar.activation(
                            KBD[q, par, m, :, r, :], QK[q, m * PN:(m + 1) * PN].rearrange("p (j n) -> p j n", j=2),
                            ACT.Identity, bias=bcol[q, ck, m:m + 1])
                ins.then_inc(k_done_a, 1)

            def evac_v(act, t, par):
                act.wait_ge(v_ready, t + 1)
                wait(act, pv_ready, 2 * (t - 1))
                if normed:
                    nc.scalar.copy(V[:, par, :, :, 0:DK],
                                   VY[:, :].rearrange("p (j h d) -> p j h d", j=2, h=H)).then_inc(v_done, 1)
                    return
                wait(act, edge_done, 2 * (t - 1))
                for j in range(2):
                    nc.scalar.copy(V[:, par, j, :, 0:DK], VB[j][:, 0:D].rearrange("p (h d) -> p h d", h=H))
                    ins = nc.scalar.copy(node_b[:, par, j, :], VB[j][:, D:DX])
                ins.then_inc(v_done, 1)

            def log_edges(act, t, par):
                wait(act, edge_done, 2 * (t - 1))
                nc.scalar.activation(log_adj[:, par, :, :].rearrange("p j n -> p (j n)"),
                                     ADJ[:, bass.ds(t * PN, PN)], ACT.Ln, bias=eps_col[:, :])\
                    .then_inc(log_done, 1)

            def evac_out(act, pair):
                act.wait_ge(ot_ready, pair + 1)
                wait(act, y_ready, pair)
                nc.scalar.copy(oT_hi[:, :, :], XO[:, :].rearrange("p (k n) -> p k n", k=KT)).then_inc(ot_hi, 1)

            def act_step(t, par):
                act = nc.scalar
                a, b, bp = 2 * (t - 1), 2 * (t - 1) + 1, 2 * (t - 1) - 1
                proj = within(t, 0, PAIRS)
                here = within(t, 1, PAIRS + 1)
                last = within(t, 2, PAIRS + 2)
                more = within(t, -1, PAIRS - 1)
                if normed:
                    if here:
                        exps(act, a, 0, 0)
                    if last:
                        evac_att(act, bp, 1)
                    if here:
                        exps(act, a, 0, 1)
                    if more:
                        evac_x(act, t + 1, 1 - par)
                    if proj:
                        evac_q(act, t, par)
                        evac_v(act, t, par)
                    if last:
                        evac_out(act, t - 2)
                    if here:
                        exps(act, b, 1, 0)
                        exps(act, b, 1, 1)
                        evac_att(act, a, 0)
                    if proj:
                        evac_k(act, t, par)
                else:
                    if proj:
                        evac_q(act, t, par)
                    if here:
                        exps(act, a, 0, 0)
                    if last:
                        evac_att(act, bp, 1)
                    if here:
                        exps(act, a, 0, 1)
                    if proj:
                        log_edges(act, t, par)
                        evac_v(act, t, par)
                        evac_k(act, t, par)
                    if here:
                        evac_att(act, a, 0)
                    if more:
                        evac_x(act, t + 1, 1 - par)
                    if here:
                        exps(act, b, 1, 0)
                        exps(act, b, 1, 1)

            def act_prog(act):
                start(act)
                evac_x(act, 0, 0)
                steps(act, 0, PAIRS + 1, 4, PAIRS - 2, act_step)
            progs["scalar"].append(act_prog)

            def add_edges(dve, g, j, epar):
                dve.wait_ge(s_ready, g + 1)
                dve.wait_ge(edge_done, g + 1)
                wait(dve, at_ready, g - 1)
                nc.vector.tensor_tensor(att[:, j, :, :], SC[:, :, :],
                                        edge_b[:, epar, j, :].unsqueeze(1).broadcast_to([P, H, N]),
                                        ALU.add).then_inc(sum_done, 1)

            def head_max(dve, g, j):
                wait(dve, exp_half, 2 * (g - 1))
                if normed:
                    dve.wait_ge(s_ready, g + 1)
                    src = SC[:, :, :]
                else:
                    dve.wait_ge(sum_done, g + 1)
                    src = att[:, j, :, :]
                nc.vector.tensor_reduce(negmax[:, j, :], src, AX.X, ALU.max, negate=True)\
                    .then_inc(max_done, 1)

            def edge_bias(dve, t, par):
                dve.wait_ge(kb_ready, t + 1)
                dve.wait_ge(log_done, t + 1)
                wait(dve, sum_done, 2 * (t - 1))
                for j in range(2):
                    nc.vector.scalar_tensor_tensor(edge_b[:, par, j, :], VB[j][:, 3 * N:4 * N],
                                                   node_b[:, par, j, 0:1], log_adj[:, par, j, :],
                                                   ALU.add, ALU.add).then_inc(edge_done, 1)

            def clip_adj(dve, t, par):
                wait(dve, mul_half, 4 * (t - 1))
                nc.vector.tensor_scalar(adjw[:, par, :, :].rearrange("p j n -> p (j n)"),
                                        ADJ[:, bass.ds(t * PN, PN)], ADJ_MIN, None, ALU.max)\
                    .then_inc(adj_ready, 1)

            def weigh(dve, g, j, t, par, hf):
                if hf == 0:
                    dve.wait_ge(adj_ready, t)
                dve.wait_ge(exp_half, 2 * g + 1 + hf)
                part = att[:, j, hf * HPT:(hf + 1) * HPT, :]
                nc.vector.tensor_tensor(part, part, adjw[:, par, j, :].unsqueeze(1).broadcast_to([P, HPT, N]),
                                        ALU.mult).then_inc(mul_half, 1)

            def norm(dve, g, j):
                dve.wait_ge(pv_ready, g + 1)
                o = PV[:, 0:H * DV].rearrange("p (h d) -> p h d", h=H)
                nc.vector.reciprocal(rsum[:, j, :], o[:, :, DK]).then_inc(rec_done, 1)
                dve.wait_ge(rec_done, g + 1)

            def finish_norm(dve, g, j, pair):
                norm(dve, g, j)
                o = PV[:, 0:H * DV].rearrange("p (h d) -> p h d", h=H)
                if normed:
                    wait(dve, ot_ready, pair)
                else:
                    wait(dve, final, g - 1)
                nc.vector.tensor_tensor(onorm[:, j, :].rearrange("p (h d) -> p h d", h=H), o[:, :, 0:DK],
                                        rsum[:, j, :].unsqueeze(2).broadcast_to([P, H, DK]),
                                        ALU.mult).then_inc(norm_done, 1)
                if not normed:
                    dve.wait_ge(norm_done, g + 1)
                    xg = X[:, bass.ds(g * D, D)]
                    nc.vector.tensor_tensor(xg, onorm[:, j, :], xg, ALU.add).then_inc(final, 1)

            def low_x(dve, i, par):
                dve.wait_ge(xt_hi, i + 1)
                nc.vector.tensor_tensor(xT_lo[:, par, :, :], XO[:, :].rearrange("p (k n) -> p k n", k=KT),
                                        xT_hi[:, par, :, :].bitcast(FP32), ALU.subtract).then_inc(xt_lo, 1)

            def residual(dve, pair):
                dve.wait_ge(y_ready, pair + 1)
                for j in range(2):
                    g = 2 * pair + j
                    wait(dve, final, g - 1)
                    nc.vector.tensor_tensor(yres[:, j, :], VY[:, j * D:(j + 1) * D],
                                            X[:, bass.ds(g * D, D)], ALU.add).then_inc(res_done, 1)

            def moments(dve, pair):
                for j in range(2):
                    g = 2 * pair + j
                    dve.wait_ge(res_done, g + 1)
                    nc.vector.bn_stats(stats[:, j, :], yres[:, j, :]).then_inc(st_done, 1)

            def aggregate_waits(dve, pair):
                dve.wait_ge(st_done, 2 * pair + 2)
                wait(dve, z_done, 2 * pair)
                wait(dve, ve_done, 2 * pair)

            def aggregate(dve, pair):
                for j in range(2):
                    nc.vector.bn_aggr(mv[:, j, :], stats[:, j, :]).then_inc(mv_done, 1)

            def center(dve, pair):
                for j in range(2):
                    g = 2 * pair + j
                    dve.wait_ge(mv_done, g + 1)
                    nc.vector.scalar_tensor_tensor(yres[:, j, :], yres[:, j, :], mv[:, j, 0:1], gamma_b[:, :],
                                                   ALU.subtract, ALU.mult).then_inc(z_done, 1)

            def scale_shift(dve, pair):
                for j in range(2):
                    g = 2 * pair + j
                    dve.wait_ge(z_done, g + 1)
                    dve.wait_ge(rstd_done, g + 1)
                    nc.vector.scalar_tensor_tensor(X[:, bass.ds(g * D, D)], yres[:, j, :], rstd[:, j, :],
                                                   beta_b[:, :], ALU.mult, ALU.add).then_inc(final, 1)

            def low_out(dve, pair):
                dve.wait_ge(ot_hi, pair + 1)
                nc.vector.tensor_tensor(oT_lo[:, :, :], XO[:, :].rearrange("p (k n) -> p k n", k=KT),
                                        oT_hi[:, :, :].bitcast(FP32), ALU.subtract).then_inc(ot_lo, 1)

            def evac_k_dve(dve, t, par):
                dve.wait_ge(k_ready, t + 1)
                wait(dve, s_ready, 2 * (t - 1))
                for m in range(KT):
                    for r in range(2, HPT):
                        q = slice(r * DK, (r + 1) * DK)
                        ins = nc.vector.tensor_scalar(
                            KBD[q, par, m, :, r, :], QK[q, m * PN:(m + 1) * PN].rearrange("p (j n) -> p j n", j=2),
                            bcol[q, ck, m:m + 1], None, ALU.add)
                ins.then_inc(k_done_v, 1)

            def dve_step(t, par):
                dve = nc.vector
                a, b, bp = 2 * (t - 1), 2 * (t - 1) + 1, 2 * (t - 1) - 1
                proj = within(t, 0, PAIRS)
                here = within(t, 1, PAIRS + 1)
                last = within(t, 2, PAIRS + 2)
                older = within(t, 3, PAIRS + 3)
                more = within(t, -1, PAIRS - 1)
                if here and not normed:
                    add_edges(dve, a, 0, 1 - par)
                if here:
                    head_max(dve, a, 0)
                if normed:
                    if older:
                        moments(dve, t - 3)
                        aggregate_waits(dve, t - 3)
                    if here:
                        weigh(dve, a, 0, t, 1 - par, 0)
                    if older:
                        aggregate(dve, t - 3)
                        center(dve, t - 3)
                    if here:
                        weigh(dve, a, 0, t, 1 - par, 1)
                    if more:
                        low_x(dve, t + 1, 1 - par)
                    if older:
                        scale_shift(dve, t - 3)
                    if proj:
                        clip_adj(dve, t, par)
                    if last:
                        finish_norm(dve, bp, 1, t - 2)
                    if here:
                        head_max(dve, b, 1)
                    if last:
                        low_out(dve, t - 2)
                    if here:
                        weigh(dve, b, 1, t, 1 - par, 0)
                    if proj:
                        evac_k_dve(dve, t, par)
                    if here:
                        weigh(dve, b, 1, t, 1 - par, 1)
                    if last:
                        residual(dve, t - 2)
                    if here:
                        finish_norm(dve, a, 0, t - 1)
                else:
                    if proj:
                        evac_k_dve(dve, t, par)
                    if last:
                        finish_norm(dve, bp, 1, t - 2)
                    if here:
                        add_edges(dve, b, 1, 1 - par)
                    if proj:
                        edge_bias(dve, t, par)
                    if here:
                        head_max(dve, b, 1)
                    if more:
                        low_x(dve, t + 1, 1 - par)
                    if here:
                        finish_norm(dve, a, 0, t - 1)

            def dve_prog(dve):
                start(dve)
                if layer == 0:
                    for c in range(CHUNKS):
                        dve.wait_ge(load_adj[c], 16)
                low_x(dve, 0, 0)
                steps(dve, 0, PAIRS + 1 + normed, 4, PAIRS - 2, dve_step)
            progs["vector"].append(dve_prog)

        def masked_layer(layer):
            L = f"{layer}"
            w = slot(W_SLOTS, "fc" + L)
            br = slot(B_SLOTS, "fc" + L)
            staged = [sem(f"staged{L}_{p}") for p in range(2)]
            xt_ready, xt_hi, xt_lo = sem("xt_ready" + L), sem("xt_hi" + L), sem("xt_lo" + L)
            v_ready, v_done = sem("v_ready" + L), sem("v_done" + L)
            kb_ready, logit_done, leaky_done = sem("kb_ready" + L), sem("logit_done" + L), sem("leaky_done" + L)
            max_done, exp_done, mask_ready = sem("max_done" + L), sem("exp_done" + L), sem("mask_ready" + L)
            pt_ready, pt_done, pv_ready, rec_done = (sem(n + L) for n in ("pt_ready", "pt_done", "pv_ready", "rec_done"))
            final = xfinal[layer]
            VB = [[QK[:, :], VY[:, :]], [SC[:, HPT:, :].rearrange("p h n -> p (h n)"), AT[:, HPT:, :].rearrange("p h n -> p (h n)")]]
            KB = SC[:, 0:2, :]
            PT = AT[:, 0:2, :]

            def start(eng):
                eng.wait_ge(xfinal[layer - 1], B)

            progs["sync"].append(lambda sp: (start(sp), stage_x(sp, layer, staged, xt_ready)))

            def transpose_x(pe, i, par):
                pe.wait_ge(staged[par], 8 * (i - par) + 16)
                wait(pe, xt_lo, i)
                for k in range(KT):
                    for j in range(2):
                        mm = nc.tensor.transpose(XO[:, k * PN + j * N:k * PN + (j + 1) * N],
                                                 xin[:, par, j, k * P:(k + 1) * P], ident[:, :])
                mm.then_inc(xt_ready, 1)

            def pe_step(t, par):
                pe = nc.tensor
                if within(t, 0, PAIRS):
                    pe.wait_ge(xt_hi, t + 1)
                    pe.wait_ge(xt_lo, t + 1)
                    wait(pe, v_done, t - 1)
                    for j in range(2):
                        mm = projected(VB[par][j][:, 0:DX], t, j, w, br, DX, par)
                    mm.then_inc(v_ready, 1)
                if within(t, 1, PAIRS + 1):
                    pe.wait_ge(v_done, t)
                    wait(pe, logit_done, 2 * (t - 1))
                    for j in range(2):
                        mm = nc.tensor.transpose(KB[:, j, :], VX[:, 1 - par, j, D + 1:D + 2].broadcast_to([P, P]),
                                                 ident[:, :])
                    mm.then_inc(kb_ready, 1)
                if within(t, 2, PAIRS + 2):
                    pe.wait_ge(exp_done, 2 * (t - 1))
                    wait(pe, pt_done, t - 2)
                    for j in range(2):
                        mm = nc.tensor.transpose(PT[:, j, :], prob[:, j, :], ident[:, :])
                    mm.then_inc(pt_ready, 1)
                if within(t, 0, PAIRS - 1):
                    transpose_x(pe, t + 1, 1 - par)
                if within(t, 2, PAIRS + 2):
                    pe.wait_ge(pt_done, t - 1)
                    wait(pe, final, 2 * (t - 2))
                    for j in range(2):
                        mm = nc.tensor.matmul(PV[:, j * D:(j + 1) * D], probT[:, j, :],
                                              VX[:, par, j, 0:D], start=True, stop=True)
                    mm.then_inc(pv_ready, 1)

            def pe_prog(pe):
                start(pe)
                transpose_x(pe, 0, 0)
                steps(pe, 0, PAIRS + 1, 4, PAIRS - 2, pe_step)
            progs["tensor"].append(pe_prog)

            def evac_x(act, i, par):
                act.wait_ge(xt_ready, i + 1)
                wait(act, v_ready, i - 1)
                nc.scalar.copy(xT_hi[:, par, :, :], XO[:, :].rearrange("p (k n) -> p k n", k=KT))\
                    .then_inc(xt_hi, 1)

            def act_step(t, par):
                act = nc.scalar
                if within(t, 2, PAIRS + 2):
                    act.wait_ge(pt_ready, t - 1)
                    wait(act, pv_ready, t - 2)
                    nc.scalar.copy(probT, PT).then_inc(pt_done, 1)
                if within(t, 0, PAIRS - 1):
                    evac_x(act, t + 1, 1 - par)
                if within(t, 1, PAIRS + 1):
                    act.wait_ge(max_done, t)
                    wait(act, pt_ready, t - 1)
                    wait(act, rec_done, t - 1)
                    for j in range(2):
                        nc.scalar.activation(prob[:, j, :], leaky[:, j, :], ACT.Exp, bias=nmax1[:, j:j + 1],
                                             accum_out=psum1[:, j:j + 1]).then_inc(exp_done, 1)
                if within(t, 0, PAIRS):
                    act.wait_ge(v_ready, t + 1)
                    wait(act, pv_ready, t - 1)
                    for j in range(2):
                        ins = nc.scalar.copy(VX[:, par, j, :], VB[par][j][:, 0:DX])
                    ins.then_inc(v_done, 1)

            def act_prog(act):
                start(act)
                evac_x(act, 0, 0)
                steps(act, 0, PAIRS + 1, 4, PAIRS - 2, act_step)
            progs["scalar"].append(act_prog)

            def low_x(dve, i, par):
                dve.wait_ge(xt_hi, i + 1)
                nc.vector.tensor_tensor(xT_lo[:, par, :, :], XO[:, :].rearrange("p (k n) -> p k n", k=KT),
                                        xT_hi[:, par, :, :].bitcast(FP32), ALU.subtract).then_inc(xt_lo, 1)

            def dve_step(t, par):
                dve = nc.vector
                if within(t, 1, PAIRS + 1):
                    wait(dve, logit_done, 2 * (t - 1))
                    nc.vector.tensor_scalar(mbias.rearrange("p j n -> p (j n)"),
                                            ADJ[:, bass.ds((t - 1) * PN, PN)], -1.0, MASKED, ALU.add, ALU.mult)\
                        .then_inc(mask_ready, 1)
                    dve.wait_ge(kb_ready, t)
                    dve.wait_ge(mask_ready, t)
                    wait(dve, leaky_done, t - 1)
                    for j in range(2):
                        nc.vector.scalar_tensor_tensor(logit[:, j, :], KB[:, j, :], VX[:, 1 - par, j, D:D + 1],
                                                       mbias[:, j, :], ALU.add, ALU.add).then_inc(logit_done, 1)
                    dve.wait_ge(logit_done, 2 * t)
                    wait(dve, exp_done, 2 * (t - 1))
                    nc.vector.scalar_tensor_tensor(leaky, logit, LEAKY, logit, ALU.mult, ALU.max)\
                        .then_inc(leaky_done, 1)
                    dve.wait_ge(leaky_done, t)
                    nc.vector.tensor_reduce(nmax1[:, :], leaky, AX.X, ALU.max, negate=True).then_inc(max_done, 1)
                if within(t, 0, PAIRS - 1):
                    low_x(dve, t + 1, 1 - par)
                if within(t, 1, PAIRS + 1):
                    dve.wait_ge(exp_done, 2 * t)
                    wait(dve, final, 2 * (t - 2))
                    nc.vector.reciprocal(prec[:, 1 - par, :], psum1[:, :]).then_inc(rec_done, 1)
                if within(t, 2, PAIRS + 2):
                    dve.wait_ge(pv_ready, t - 1)
                    dve.wait_ge(rec_done, t - 1)
                    for j in range(2):
                        xg = X[:, bass.ds((2 * (t - 2) + j) * D, D)]
                        nc.vector.scalar_tensor_tensor(xg, PV[:, j * D:(j + 1) * D], prec[:, par, j:j + 1], xg,
                                                       ALU.mult, ALU.add).then_inc(final, 1)

            def dve_prog(dve):
                start(dve)
                low_x(dve, 0, 0)
                steps(dve, 0, PAIRS + 1, 4, PAIRS - 2, dve_step)
            progs["vector"].append(dve_prog)

        def stores(sp):
            with sp.Fori(0, PAIRS) as i:
                sp.wait_ge(xfinal[3], 2 * i + 2)
                sp.dma_start(out[bass.ds(i * 2, 2)].rearrange("g p d -> p g d"),
                             X[:, bass.ds(i * 2 * D, 2 * D)].rearrange("p (g d) -> p g d", g=2))\
                    .then_inc(stored, 16)
            sp.wait_ge(stored, 16 * PAIRS)

        progs["sync"].append(sync_prep)
        progs["scalar"].append(scalar_prep)
        progs["gpsimd"].append(gpsimd_prep)
        progs["tensor"].append(tensor_prep)
        progs["vector"].append(vector_prep)
        attention(0)
        masked_layer(1)
        attention(2)
        masked_layer(3)
        progs["sync"].append(stores)

        @block.sync
        def _(sp):
            for part in progs["sync"]:
                part(sp)

        @block.gpsimd
        def _(pool):
            for part in progs["gpsimd"]:
                part(pool)

        @block.scalar
        def _(act):
            for part in progs["scalar"]:
                part(act)

        @block.tensor
        def _(pe):
            for part in progs["tensor"]:
                part(pe)

        @block.vector
        def _(dve):
            for part in progs["vector"]:
                part(dve)


def kernel(**inputs):
    import numpy as np
    import concourse.bacc as bacc
    from concourse.bass_utils import run_bass_kernel_spmd

    a = {k: np.asarray(v) for k, v in inputs.items()}

    def tiles(w):
        return w.reshape(2, 128, -1).transpose(1, 0, 2)

    fwd = [a["L0_gnn_Wq"].T, a["L0_gnn_Wk"].T, a["L0_gnn_Wv"].T, a["L0_gnn_Wo"].T, a["L1_gnn_fc_w"].T,
           a["L2_gnn_W_q"], a["L2_gnn_W_k"], a["L2_gnn_W_v"], a["L3_gnn_W_fc"]]
    rev = [a["L1_gnn_fc_w"], a["L3_gnn_W_fc"].T]
    qkw = [np.stack([a["L1_gnn_q_w"][0], a["L1_gnn_k_w"][0]], 1),
           np.concatenate([a["L3_gnn_w_q"], a["L3_gnn_w_k"]], 1)]
    cols = [a[n] for n in ("L0_gnn_bq", "L0_gnn_bk", "L2_gnn_b_q", "L2_gnn_b_k", "L1_gnn_fc_b", "L3_gnn_b_fc")]
    rows = [a[n] for n in ("L0_gnn_bv", "L0_gnn_bo", "L1_gnn_fc_b", "L2_gnn_b_v", "L3_gnn_b_fc")]
    arrays = {
        "x": a["x"], "adj": a["adj"],
        "weights": np.stack([tiles(w) for w in fwd], 1),
        "fc_rev": np.stack([tiles(w) for w in rev], 1),
        "qk_w": np.stack([tiles(w) for w in qkw], 1),
        "bias_cols": np.stack([tiles(c)[:, :, 0] for c in cols], 1),
        "bias_rows": np.stack(rows, 0),
        "qk_b": np.stack([np.concatenate([a["L1_gnn_q_b"], a["L1_gnn_k_b"]]),
                          np.concatenate([a["L3_gnn_b_q"], a["L3_gnn_b_k"]])], 0),
        "gamma": a["L0_gnn_gamma"], "beta": a["L0_gnn_beta"],
        "w_g": tiles(a["L2_gnn_w_g"].reshape(2, D).T), "b_g": a["L2_gnn_b_g"].reshape(1),
        "eye": np.eye(128, dtype=np.float32),
    }
    nc = bacc.Bacc("TRN2", target_bir_lowering=False, num_devices=1)
    arrays = {"in_" + k: np.ascontiguousarray(v) for k, v in arrays.items()}
    args = [nc.dram_tensor(k, v.shape, mybir.dt.from_np(v.dtype), kind="ExternalInput").ap()
            for k, v in arrays.items()]
    out = nc.dram_tensor("out", [B, N, D], FP32, kind="ExternalOutput").ap()
    build(nc, *args, out)
    r = run_bass_kernel_spmd(nc, [arrays], core_ids=[0])
    return r.results[0]["out"]
```

```python
from contextlib import ExitStack

import concourse.bass as bass
from concourse import mybir

FP32 = mybir.dt.float32
FP32R = mybir.dt.float32r
BF16 = mybir.dt.bfloat16
ALU = mybir.AluOpType
ACT = mybir.ActivationFunctionType
AX = mybir.AxisListType

B, N, D, H = 64, 128, 256, 8
DK = D // H
P = 128
KT = D // P
HPT = P // DK
HPR = HPT // 2
PAIRS = B // 2
PN = 2 * N
DX = D + 2
LATE = 4
BEHIND = 5
CHUNKS = 8
LN_EPS = 1e-05
ADJ_MIN = 1e-08
ADJ_EPS = 1e-09
MASKED = 1e9
LEAKY = 0.01
W_SLOTS = ["q0", "k0", "v0", "o0", "fc1", "q2", "k2", "v2", "fc3"]
B_SLOTS = ["v0", "o0", "fc1", "v2", "fc3"]


def wait(eng, sem, value):
    if isinstance(value, int) and value <= 0:
        return
    eng.wait_ge(sem, value)


def steps(eng, first, last, even_first, even_end, emit):
    for t in range(first, even_first):
        emit(t, t % 2)
    with eng.Fori(even_first, even_end - 1, 2) as t:
        emit(t, 0)
        emit(t + 1, 1)
    for t in range(even_end, last + 1):
        emit(t, t % 2)


def head(s):
    half, m, r = s // HPT, s % HPT // HPR, s % HPR
    return m * HPT + half * HPR + r


def place(h):
    return [head(s) for s in range(H)].index(h)


def within(t, lo, hi):
    return not isinstance(t, int) or lo <= t < hi


def build(nc, x, adj, weights, fc_rev, qk_w, bias_cols, bias_rows, qk_b, gamma, beta, w_g, b_g, eye, out):
    ctx = ExitStack()
    with ctx:
        def sb(name, shape, dt=FP32):
            return ctx.enter_context(nc.sbuf_tensor(name, shape, dt))

        def sem(name):
            return ctx.enter_context(nc.semaphore(name))

        X = sb("X", [P, B * D])
        ADJ = sb("ADJ", [P, B * N])
        w_hi = sb("w_hi", [P, len(W_SLOTS), KT, DX], FP32R)
        w_lo = sb("w_lo", [P, len(W_SLOTS), KT, DX], FP32R)
        ident = sb("ident", [P, P])
        bcol = sb("bcol", [P, 4, KT])
        brow = sb("brow", [96, len(B_SLOTS), DX], BF16)
        ones3 = sb("ones3", [96, P], BF16)
        gamma_b = sb("gamma_b", [P, D])
        beta_b = sb("beta_b", [P, D])
        xin = sb("xin", [P, 2, 2, D])
        xT_hi = sb("xT_hi", [P, 2, KT, PN], FP32R)
        xT_lo = sb("xT_lo", [P, 2, KT, PN], FP32R)
        QT = sb("QT", [P, 2, KT, PN])
        KBD = sb("KBD", [P, 2, KT, HPR, PN])
        block_mask = sb("block_mask", [P, HPR])
        V = sb("V", [P, 2, 2, H, DK])
        negmax = sb("negmax", [P, 2, H])
        node_b = sb("node_b", [P, 2, 2, 2])
        log_adj = sb("log_adj", [P, 2, 2, N])
        edge_b = sb("edge_b", [P, 2, 2, N])
        att = sb("att", [P, 2, H, N])
        attT = sb("attT", [P, 2, H, N])
        asum = sb("asum", [P, 2, H])
        rsum = sb("rsum", [P, 2, H])
        oT = sb("oT", [P, KT, PN])
        onorm = sb("onorm", [P, 2, D])
        oT_hi = sb("oT_hi", [P, KT, PN], FP32R)
        oT_lo = sb("oT_lo", [P, KT, PN], FP32R)
        yres = sb("yres", [P, 2, D])
        stats = sb("stats", [P, 2, 6])
        mv = sb("mv", [P, 2, 2])
        veps = sb("veps", [P, 2, 1])
        rstd = sb("rstd", [P, 2, 1])
        mhalf = sb("mhalf", [P, 1])
        eps_col = sb("eps_col", [P, 1])
        ln_eps = sb("ln_eps", [P, 1])
        zero_col = sb("zero_col", [P, 1])
        spare = att[:, :, :, :].rearrange("p a h n -> p (a h n)")
        VX = spare[:, 0:4 * DX].rearrange("p (a j d) -> p a j d", a=2, j=2)
        mbias, logit, leaky = (spare[:, 4 * DX + n * PN:4 * DX + (n + 1) * PN].rearrange("p (j n) -> p j n", j=2)
                               for n in range(3))
        prob, probT = attT[:, 0, 0:2, :], attT[:, 0, 2:4, :]
        nmax1 = sb("nmax1", [P, 2])
        psum1 = sb("psum1", [P, 2])
        prec = sb("prec", [P, 2, 2])

        bank = [ctx.enter_context(nc.psum_tensor(f"bank{n}", [P, 512], FP32)) for n in range(4)]
        SC = ctx.enter_context(nc.psum_tensor("SC", [P, H, N], FP32))
        AT = ctx.enter_context(nc.psum_tensor("AT", [P, H, N], FP32))
        XO, QK, VY, PV = bank

        load_x = [sem(f"load_x{c}") for c in range(CHUNKS)]
        load_adj = [sem(f"load_adj{c}") for c in range(CHUNKS)]
        load_w = [sem("load_w_first"), sem("load_w_rest")]
        load_first = sem("load_first")
        load_c = sem("load_c")
        prep_p = sem("prep_p")
        prep_v = sem("prep_v")
        prep_t = sem("prep_t")
        prep_hi = sem("prep_hi")
        prep_rows = sem("prep_rows")
        prep_rest = sem("prep_rest")
        marked = sem("marked")
        rest_rows = sem("rest_rows")
        prepared = sem("prepared")
        prepared_rest = sem("prepared_rest")
        stored = sem("stored")
        xfinal = [sem(f"xfinal{l}") for l in range(4)]

        G = B // CHUNKS
        Xg = X[:, :].rearrange("p (g d) -> p g d", d=D)
        Ag = ADJ[:, :].rearrange("p (g n) -> p g n", n=N)

        free_at = [LATE * G * D]

        def early(rows, *shape):
            n = 1
            for s in shape:
                n *= s
            at = free_at[0]
            free_at[0] = at + n
            letters = "abcd"[:len(shape)]
            return X[0:rows, at:at + n].rearrange(f"p ({' '.join(letters)}) -> p {' '.join(letters)}",
                                                  **dict(zip(letters, shape)))

        w_raw = early(P, len(W_SLOTS), KT, D)
        wg_raw = early(P, KT, 2)
        qkw = early(P, 2, KT, 2)
        bfc = early(P, 2, KT)
        qkb = early(96, 2, 2)
        bg = early(96, 1)
        row_raw = early(96, len(B_SLOTS), DX)
        row_res = early(96, len(B_SLOTS), DX)
        fc_raw = att[:, :, :, :].rearrange("p a h n -> p (a h n)")[:, 0:2 * KT * D]\
            .rearrange("p (f t d) -> p f t d", f=2, t=KT)
        row_part = sb("row_part", [96, len(B_SLOTS), DX], BF16)

        def slot(names, name):
            return names.index(name)

        FC = [slot(W_SLOTS, "fc1"), slot(W_SLOTS, "fc3")]
        WV2 = slot(W_SLOTS, "v2")
        W0, B0 = slot(W_SLOTS, "fc1"), slot(B_SLOTS, "fc1")
        FB = [slot(B_SLOTS, "fc1"), slot(B_SLOTS, "fc3")]

        block = ctx.enter_context(nc.Block())
        progs = {"sync": [], "gpsimd": [], "scalar": [], "tensor": [], "vector": []}

        def load_chunk(sp, c):
            if c == LATE:
                sp.wait_ge(prepared_rest, PREPARED_REST)
                sp.wait_ge(rest_rows, REST_ROWS)
            sp.dma_start(Xg[:, G * c:G * (c + 1), :],
                         x[G * c:G * (c + 1)].rearrange("g p d -> p g d")).then_inc(load_x[c], 16)
            sp.dma_start(Ag[:, G * c:G * (c + 1), :],
                         adj[G * c:G * (c + 1)].rearrange("g p n -> p g n")).then_inc(load_adj[c], 16)

        def sync_prep(sp):
            sp.dma_start(w_raw[:, 0:W0], weights[:, 0:W0]).then_inc(load_w[0], 16)

        def scalar_prep(act):
            act.dma_start(row_raw[:, :, 0:D], bias_rows.partition_broadcast(96)).then_inc(load_first, 16)
            act.dma_start(ident[:, :], eye).then_inc(load_first, 16)
            act.dma_start(bcol[:, :, :], bias_cols[:, 0:4, :]).then_inc(load_first, 16)
            act.dma_start(fc_raw, fc_rev).then_inc(load_c, 16)
            act.dma_start(qkw, qk_w).then_inc(load_c, 16)
            act.dma_start(bfc, bias_cols[:, 4:6, :]).then_inc(load_c, 16)
            act.dma_start(qkb, qk_b.partition_broadcast(96)).then_inc(load_c, 16)
            act.dma_start(gamma_b[:, :], gamma.partition_broadcast(P)).then_inc(load_c, 16)
            act.dma_start(beta_b[:, :], beta.partition_broadcast(P)).then_inc(load_c, 16)
            act.dma_start(wg_raw, w_g).then_inc(load_c, 16)
            act.dma_start(bg, b_g.partition_broadcast(96)).then_inc(load_c, 16)
            nc.scalar.preload_act_table_set("natural_log_exp_and_others")
            act.wait_ge(load_first, 3 * 16)
            for s in (0, 2):
                nc.scalar.mul(bcol[:, s, :], bcol[:, s, :], float(DK) ** -0.5).then_inc(prepared, 1)

        def scalar_prep_rest(act):
            act.wait_ge(load_w[1], 16)
            nc.scalar.copy(w_hi[:, W0:, :, 0:D], w_raw[:, W0:]).then_inc(prep_hi, 1)

        def split_rows(eng, queue, own, n, slots, cols, done):
            src = row_raw
            for r in range(3):
                eng.tensor_copy(row_part[:, slots, cols], src[:, slots, cols]).then_inc(own, 1)
                n += 1
                queue.wait_ge(own, n)
                eng.tensor_copy(brow[32 * r:32 * r + 32, slots, cols],
                                row_part[32 * r:32 * r + 32, slots, cols]).then_inc(done, 1)
                if eng is nc.gpsimd:
                    queue.wait_ge(done, r + 1)
                if r == 2:
                    return n
                eng.tensor_tensor(row_res[:, slots, cols], src[:, slots, cols], row_part[:, slots, cols],
                                  ALU.subtract).then_inc(own, 1)
                n += 1
                queue.wait_ge(own, n)
                src = row_res

        def gpsimd_prep(pool):
            nc.gpsimd.memset(zero_col[:, :], 0.0).then_inc(prepared, 1)
            nc.gpsimd.memset(mhalf[:, :], -0.5).then_inc(prepared, 1)
            nc.gpsimd.memset(eps_col[:, :], ADJ_EPS).then_inc(prepared, 1)
            nc.gpsimd.memset(ln_eps[:, :], LN_EPS).then_inc(prepared, 1)
            nc.gpsimd.memset(block_mask[:, :], 0.0).then_inc(prep_p, 1)
            nc.gpsimd.memset(row_raw[:, :, D:DX], 0.0).then_inc(prep_p, 1)
            nc.gpsimd.memset(ones3[:, :], 0.0).then_inc(prep_p, 1)
            pool.wait_ge(prep_p, 3)
            for h in range(HPT):
                nc.gpsimd.memset(block_mask[h * DK:(h + 1) * DK, h % HPR:h % HPR + 1], 1.0).then_inc(marked, 1)
            for r in (0, 32, 64):
                nc.gpsimd.memset(ones3[r:r + 1, :], 1.0).then_inc(marked, 1)
            pool.wait_ge(marked, MARKED)
            pool.wait_ge(load_first, 3 * 16)
            n = split_rows(nc.gpsimd, pool, prep_rest, 0, slice(B0, len(B_SLOTS)), slice(0, D), rest_rows)
            pool.wait_ge(prep_hi, 1)
            nc.gpsimd.tensor_tensor(w_lo[:, W0:, :, 0:D], w_raw[:, W0:],
                                    w_hi[:, W0:, :, 0:D].bitcast(FP32), ALU.subtract).then_inc(prepared_rest, 1)
            pool.wait_ge(load_c, 8 * 16)
            nc.gpsimd.tensor_copy(w_hi[:, WV2, :, D:DX], wg_raw).then_inc(prep_rest, 1)
            pool.wait_ge(prep_rest, n + 1)
            nc.gpsimd.tensor_tensor(w_lo[:, WV2, :, D:DX], wg_raw, w_hi[:, WV2, :, D:DX].bitcast(FP32),
                                    ALU.subtract).then_inc(prepared_rest, 1)

        def tensor_prep(pe):
            pe.wait_ge(load_c, 8 * 16)
            for f in range(2):
                for m in range(KT):
                    for t in range(KT):
                        mm = nc.tensor.matmul(AT[:, 0, 4 * f + 2 * m:4 * f + 2 * m + 2],
                                              fc_raw[:, f, t, m * P:(m + 1) * P], qkw[:, f, t, :],
                                              start=(t == 0), stop=(t == KT - 1))
            mm.then_inc(prep_t, 1)
            for f in range(2):
                for t in range(KT):
                    mm = nc.tensor.matmul(AT[0:96, HPT, 2 * f:2 * f + 2],
                                          bfc[:, f, t:t + 1].broadcast_to([P, 96]), qkw[:, f, t, :],
                                          start=(t == 0), stop=(t == KT - 1))
            mm.then_inc(prep_t, 1)

        def vector_prep(dve):
            dve.wait_ge(load_w[0], 16)
            nc.vector.tensor_copy(w_hi[:, 0:W0, :, 0:D], w_raw[:, 0:W0]).then_inc(prep_v, 1)
            dve.wait_ge(prep_v, 1)
            nc.vector.tensor_tensor(w_lo[:, 0:W0, :, 0:D], w_raw[:, 0:W0],
                                    w_hi[:, 0:W0, :, 0:D].bitcast(FP32), ALU.subtract).then_inc(prepared, 1)
            dve.wait_ge(prep_p, 3)
            dve.wait_ge(load_first, 3 * 16)
            split_rows(nc.vector, dve, prep_v, 1, slice(0, B0), slice(0, D), prepared)

        def vector_prep_rest(dve):
            n = 1 + 5
            dve.wait_ge(prep_t, 2)
            for f in range(2):
                raw = AT[:, 0, 4 * f:4 * f + 4].rearrange("p (m c) -> p m c", c=2)
                nc.vector.tensor_copy(w_hi[:, FC[f], :, D:DX], raw).then_inc(prep_v, 1)
                n += 1
                dve.wait_ge(prep_v, n)
                nc.vector.tensor_tensor(w_lo[:, FC[f], :, D:DX], raw,
                                        w_hi[:, FC[f], :, D:DX].bitcast(FP32), ALU.subtract).then_inc(prepared_rest, 1)
                nc.vector.tensor_tensor(row_raw[:, FB[f], D:DX], AT[0:96, HPT, 2 * f:2 * f + 2], qkb[:, f, :],
                                        ALU.add).then_inc(prep_rows, 1)
            nc.vector.tensor_copy(row_raw[:, slot(B_SLOTS, "v2"), D:D + 1], bg).then_inc(prep_rows, 1)
            dve.wait_ge(prep_rows, 3)
            split_rows(nc.vector, dve, prep_v, n, slice(B0, len(B_SLOTS)), slice(D, DX), prepared_rest)

        MARKED = HPT + 3
        REST_ROWS = 3
        PREPARED = 2 + 4 + 3 + 1
        PREPARED_REST = 1 + 1 + 2 + 3

        def matmul3(o, l_hi, l_lo, r_hi, r_lo, start, stop):
            nc.tensor.matmul(o, l_hi, r_hi, start=start, stop=False)
            nc.tensor.matmul(o, l_lo, r_hi, start=False, stop=False)
            return nc.tensor.matmul(o, l_hi, r_lo, start=False, stop=stop)

        def projected(o, t, j, w, b, cols, par):
            nc.tensor.matmul(o, ones3[:, :], brow[:, b, 0:cols], start=True, stop=False)
            for k in range(KT):
                mm = matmul3(o, xT_hi[:, par, k, j * N:(j + 1) * N], xT_lo[:, par, k, j * N:(j + 1) * N],
                             w_hi[:, w, k, 0:cols], w_lo[:, w, k, 0:cols], False, k == KT - 1)
            return mm

        def store(sp, i):
            sp.wait_ge(xfinal[3], 2 * i + 2)
            sp.dma_start(out[bass.ds(i * 2, 2)].rearrange("g p d -> p g d"),
                         X[:, bass.ds(i * 2 * D, 2 * D)].rearrange("p (g d) -> p g d", g=2)).then_inc(stored, 16)

        def stage_x(sp, layer, staged, xt_ready):
            def one(i, par):
                wait(sp, xt_ready, i - 1)
                if layer:
                    wait(sp, xfinal[layer - 1], 2 * i + 2)
                sp.dma_start(xin[:, par, :, :].rearrange("p a d -> p (a d)"),
                             X[:, bass.ds(i * 2 * D, 2 * D)]).then_inc(staged[par], 16)
            if layer == 0:
                per = PAIRS // CHUNKS
                for i in range(2):
                    sp.dma_start(xin[:, i, :, :], x[2 * i:2 * i + 2].rearrange("g p d -> p g d"))\
                        .then_inc(staged[i], 16)
                load_chunk(sp, 0)
                sp.dma_start(w_raw[:, W0:], weights[:, W0:]).then_inc(load_w[1], 16)
                for c in range(CHUNKS):
                    sp.wait_ge(load_x[c], 16)
                    sp.wait_ge(load_adj[c], 16)
                    for i in range(max(c * per, 2), (c + 1) * per):
                        one(i, i % 2)
                        if i == c * per + 2 and c + 1 < CHUNKS:
                            load_chunk(sp, c + 1)
            elif layer < 3:
                steps(sp, 0, PAIRS - 1, 2, PAIRS, one)
            else:
                def one_and_store(i, par):
                    if within(i, 0, PAIRS):
                        one(i, par)
                    if within(i, BEHIND, PAIRS + BEHIND):
                        store(sp, i - BEHIND)
                steps(sp, 0, PAIRS + BEHIND - 1, BEHIND + BEHIND % 2, PAIRS, one_and_store)

        def attention(layer, before=None):
            L = f"{layer}"
            normed = layer == 0
            wq, wk, wv = (slot(W_SLOTS, c + L) for c in "qkv")
            bv = slot(B_SLOTS, "v" + L)
            cq, ck = (0, 1) if layer == 0 else (2, 3)
            staged = [sem(f"staged{L}_{p}") for p in range(2)]
            xt_ready, xt_hi, xt_lo = sem("xt_ready" + L), sem("xt_hi" + L), sem("xt_lo" + L)
            q_ready, q_done = sem("q_ready" + L), sem("q_done" + L)
            k_ready, k_done = sem("k_ready" + L), sem("k_done" + L)
            v_ready, v_done, nodes_done = sem("v_ready" + L), sem("v_done" + L), sem("nodes_done" + L)
            s_ready, max_done = sem("s_ready" + L), sem("max_done" + L)
            exp_half, scale_half = sem("exp_half" + L), sem("scale_half" + L)
            at_ready, at_done = sem("at_ready" + L), sem("at_done" + L)
            pv_ready, rec_done, norm_done = sem("pv_ready" + L), sem("rec_done" + L), sem("norm_done" + L)
            adj_ready = sem("adj_ready" + L)
            ot_hi, ot_lo = sem("ot_hi" + L), sem("ot_lo" + L)
            y_ready, res_done, st_done = sem("y_ready" + L), sem("res_done" + L), sem("st_done" + L)
            mv_done, ve_done, rstd_done = sem("mv_done" + L), sem("ve_done" + L), sem("rstd_done" + L)
            z_done = sem("z_done" + L)
            log_done, kb_ready, edge_done = sem("log_done" + L), sem("kb_ready" + L), sem("edge_done" + L)
            sum_done, copied, back_ready = sem("sum_done" + L), sem("copied" + L), sem("back_ready" + L)
            VB = [VY, XO]
            OB = [PV[:, D:2 * D], VY[:, 0:D]]
            final = xfinal[layer]

            def start(eng):
                if layer:
                    eng.wait_ge(before[1], B)
                    eng.wait_ge(prepared_rest, PREPARED_REST)
                    eng.wait_ge(rest_rows, REST_ROWS)
                else:
                    eng.wait_ge(prepared, PREPARED)
                    eng.wait_ge(marked, MARKED)

            def sync_prog(sp):
                if layer:
                    sp.wait_ge(before[0], PAIRS)
                stage_x(sp, layer, staged, xt_ready)
            progs["sync"].append(sync_prog)

            def scale(g, j, hf):
                wait(nc.gpsimd, rec_done, 2 * g + 1 + hf)
                part = slice(hf * HPT, (hf + 1) * HPT)
                nc.gpsimd.tensor_tensor(att[:, j, part, :], att[:, j, part, :],
                                        rsum[:, j, part].unsqueeze(2).broadcast_to([P, HPT, N]),
                                        ALU.mult).then_inc(scale_half, 1)

            def add_x(t, par):
                for j in range(2):
                    g = 2 * t + j
                    xg = X[:, bass.ds(g * D, D)]
                    wait(nc.gpsimd, norm_done, g + 1)
                    nc.gpsimd.tensor_tensor(xg, onorm[:, j, :], xg, ALU.add).then_inc(final, 1)

            def pool_step(t, par):
                here = within(t, 1, PAIRS + 1)
                for j in range(2):
                    if here:
                        scale(2 * (t - 1) + j, j, 0)
                        scale(2 * (t - 1) + j, j, 1)
                    if j == 0 and within(t, 3, PAIRS + 3):
                        inverse_std(t - 3)

            def inverse_std(t):
                for j in range(2):
                    g = 2 * t + j
                    wait(nc.gpsimd, mv_done, g + 1)
                    nc.gpsimd.tensor_tensor(veps[:, j, :], mv[:, j, 1:2], ln_eps[:, :], ALU.add)\
                        .then_inc(ve_done, 1)
                    wait(nc.gpsimd, ve_done, g + 1)
                    wait(nc.gpsimd, final, g - 1)
                    nc.gpsimd.tensor_tensor(rstd[:, j, :], veps[:, j, :], mhalf[:, :], ALU.pow)\
                        .then_inc(rstd_done, 1)

            def pool_prog(pool):
                if normed:
                    start(pool)
                    steps(pool, 1, PAIRS + 2, 4, PAIRS - 2, pool_step)
                else:
                    steps(pool, 0, PAIRS - 1, 2, PAIRS, add_x)
            progs["gpsimd"].append(pool_prog)

            def transpose_x(pe, i, par):
                pe.wait_ge(staged[par], 8 * (i - par) + 16)
                wait(pe, xt_lo, i)
                if normed:
                    wait(pe, res_done, 2 * (i - 3))
                else:
                    wait(pe, v_done, i)
                for k in range(KT):
                    for j in range(2):
                        mm = nc.tensor.transpose(XO[:, k * PN + j * N:k * PN + (j + 1) * N],
                                                 xin[:, par, j, k * P:(k + 1) * P], ident[:, :])
                mm.then_inc(xt_ready, 1)

            def project_out(pe, pair):
                pe.wait_ge(ot_hi, 2 * pair + 2)
                pe.wait_ge(ot_lo, 2 * pair + 2)
                wait(pe, xt_lo, pair + 4 if not isinstance(pair, int) else min(pair + 4, PAIRS))
                wo = slot(W_SLOTS, "o0")
                for j in range(2):
                    o = XO[:, j * D:(j + 1) * D]
                    nc.tensor.matmul(o, ones3[:, :], brow[:, slot(B_SLOTS, "o0"), 0:D], start=True, stop=False)
                    for k in range(KT):
                        mm = matmul3(o, oT_hi[:, k, j * N:(j + 1) * N], oT_lo[:, k, j * N:(j + 1) * N],
                                     w_hi[:, wo, k, 0:D], w_lo[:, wo, k, 0:D], False, k == KT - 1)
                mm.then_inc(y_ready, 1)

            def project_v(pe, t, par):
                if not normed:
                    wait(pe, xt_lo, t + 1)
                    wait(pe, norm_done, 2 * (t - 2))
                wait(pe, v_done, t)
                for j in range(2):
                    o = VY[:, j * D:(j + 1) * D] if normed else VB[j][:, 0:DX]
                    mm = projected(o, t, j, wv, bv, D if normed else DX, par)
                mm.then_inc(v_ready, 1)

            def spread_keys(pe, t, par):
                pe.wait_ge(nodes_done, t + 1)
                for j in range(2):
                    mm = nc.tensor.transpose(VB[j][:, 3 * N:4 * N],
                                             node_b[:, par, j, 1:2].broadcast_to([P, P]), ident[:, :])
                mm.then_inc(kb_ready, 1)

            def project_t(o_bank, w, par, ready):
                for m in range(KT):
                    for k in range(KT):
                        mm = matmul3(o_bank[:, m * PN:(m + 1) * PN],
                                     w_hi[:, w, k, m * P:(m + 1) * P], w_lo[:, w, k, m * P:(m + 1) * P],
                                     xT_hi[:, par, k, :], xT_lo[:, par, k, :], k == 0, k == KT - 1)
                mm.then_inc(ready, 1)

            def scores(pe, g, j, par):
                wait(pe, sum_done, g)
                for m in range(KT):
                    for half in range(2):
                        rows = slice(half * HPR * DK, (half + 1) * HPR * DK)
                        at = half * HPT + m * HPR
                        mm = nc.tensor.matmul(SC[:, at:at + HPR, :],
                                              QT[rows, par, m, j * N:(j + 1) * N],
                                              KBD[rows, par, m, :, j * N:(j + 1) * N],
                                              start=True, stop=True)
                mm.then_inc(s_ready, 1)

            def transpose_att(pe, g, j):
                wait(pe, scale_half if normed else exp_half, 2 * g + 2)
                wait(pe, at_done, g)
                for h in range(H):
                    mm = nc.tensor.transpose(AT[:, h, :], att[:, j, h, :], ident[:, :])
                mm.then_inc(at_ready, 1)

            def values(pe, g, j, par):
                wait(pe, at_done, g + 1)
                if normed:
                    wait(pe, ot_lo, g)
                else:
                    wait(pe, copied if j == 0 else norm_done, g)
                for h in range(H):
                    m, r = h // HPT, h % HPT
                    mm = nc.tensor.matmul(PV[r * DK:(r + 1) * DK, m * N:(m + 1) * N], V[:, par, j, h, :],
                                          attT[:, j, place(h), :], start=True, stop=True)
                mm.then_inc(pv_ready, 1)

            def transpose_back(pe, pair, g, j):
                wait(pe, copied, g + 1)
                if j == 1:
                    pe.wait_ge(v_done, pair + 3 if not isinstance(pair, int) else min(pair + 3, PAIRS))
                for m in range(KT):
                    mm = nc.tensor.transpose(OB[j][:, m * P:(m + 1) * P], oT[:, m, j * N:(j + 1) * N],
                                             ident[:, :])
                mm.then_inc(back_ready, 1)

            def pe_step(t, par):
                pe = nc.tensor
                a, b, bp = 2 * (t - 1), 2 * (t - 1) + 1, 2 * (t - 1) - 1
                proj = within(t, 0, PAIRS)
                here = within(t, 1, PAIRS + 1)
                last = within(t, 2, PAIRS + 2)
                older = within(t, 3, PAIRS + 3)
                more = within(t, -1, PAIRS - 1)
                if here:
                    pe.wait_ge(q_done, t)
                    pe.wait_ge(k_done, t)
                    scores(pe, a, 0, 1 - par)
                if proj:
                    pe.wait_ge(xt_hi, t + 1)
                    pe.wait_ge(xt_lo, t + 1)
                    wait(pe, k_done, t)
                    project_t(QK, wq, par, q_ready)
                if normed:
                    if older:
                        project_out(pe, t - 3)
                    if proj:
                        project_v(pe, t, par)
                    if last:
                        pe.wait_ge(v_done, t - 1)
                        values(pe, bp - 1, 0, par)
                        transpose_att(pe, bp, 1)
                    if here:
                        scores(pe, b, 1, 1 - par)
                    if proj:
                        pe.wait_ge(q_done, t + 1)
                        project_t(QK, wk, par, k_ready)
                    if more:
                        transpose_x(pe, t + 1, 1 - par)
                    if last:
                        values(pe, bp, 1, par)
                    if here:
                        transpose_att(pe, a, 0)
                else:
                    if proj:
                        project_v(pe, t, par)
                    if last:
                        pe.wait_ge(v_done, t - 1)
                        values(pe, bp - 1, 0, par)
                        transpose_att(pe, bp, 1)
                        transpose_back(pe, t - 2, bp - 1, 0)
                    if here:
                        scores(pe, b, 1, 1 - par)
                    if proj:
                        spread_keys(pe, t, par)
                        pe.wait_ge(q_done, t + 1)
                        project_t(QK, wk, par, k_ready)
                    if last:
                        values(pe, bp, 1, par)
                    if here:
                        transpose_att(pe, a, 0)
                    if more:
                        transpose_x(pe, t + 1, 1 - par)
                    if last:
                        transpose_back(pe, t - 2, bp, 1)

            def pe_prog(pe):
                start(pe)
                transpose_x(pe, 0, 0)
                if normed:
                    pe_step(0, 0)
                    tensor_prep(pe)
                steps(pe, 1 if normed else 0, PAIRS + 1 + normed, 4, PAIRS - 2, pe_step)
            progs["tensor"].append(pe_prog)

            def exps(act, g, j, hf):
                if hf == 0:
                    act.wait_ge(max_done, g + 1)
                    wait(act, at_ready, g - 1)
                    wait(act, rec_done, 2 * (g - 1) if normed else g - 1)
                for s in range(hf * HPT, (hf + 1) * HPT):
                    at = s if normed else head(s)
                    ins = nc.scalar.activation(att[:, j, s, :], att[:, j, s, :], ACT.Exp,
                                               bias=negmax[:, j, s:s + 1], accum_out=asum[:, j, at:at + 1])
                ins.then_inc(exp_half, 1)

            def evac_att(act, g, j):
                act.wait_ge(at_ready, g + 1)
                wait(act, pv_ready, g - 1)
                nc.scalar.copy(attT[:, j, :, :], AT[:, :, :]).then_inc(at_done, 1)

            def evac_x(act, i, par):
                act.wait_ge(xt_ready, i + 1)
                wait(act, k_ready, i - 1)
                wait(act, v_ready, i - 1)
                nc.scalar.copy(xT_hi[:, par, :, :], XO[:, :].rearrange("p (k n) -> p k n", k=KT))\
                    .then_inc(xt_hi, 1)

            def evac_q(act, t, par):
                act.wait_ge(q_ready, t + 1)
                wait(act, s_ready, 2 * (t - 1))
                for m in range(KT):
                    ins = nc.scalar.activation(QT[:, par, m, :], QK[:, m * PN:(m + 1) * PN], ACT.Identity,
                                               bias=bcol[:, cq, m:m + 1], scale=float(DK) ** -0.5)
                ins.then_inc(q_done, 1)

            def evac_v(act, t, par):
                act.wait_ge(v_ready, t + 1)
                wait(act, pv_ready, 2 * (t - 1))
                if normed:
                    nc.scalar.copy(V[:, par, :, :, 0:DK],
                                   VY[:, :].rearrange("p (j h d) -> p j h d", j=2, h=H)).then_inc(v_done, 1)
                    return
                act.wait_ge(edge_done, 2 * t + 2)
                for j in range(2):
                    ins = nc.scalar.copy(V[:, par, j, :, 0:DK], VB[j][:, 0:D].rearrange("p (h d) -> p h d", h=H))
                ins.then_inc(v_done, 1)

            def evac_nodes(act, t, par):
                act.wait_ge(v_ready, t + 1)
                wait(act, edge_done, 2 * (t - 1))
                for j in range(2):
                    ins = nc.scalar.copy(node_b[:, par, j, :], VB[j][:, D:DX])
                ins.then_inc(nodes_done, 1)

            def log_edges(act, t, par):
                if normed:
                    act.wait_ge(adj_ready, t + 1)
                    wait(act, sum_done, 2 * (t - 1))
                    nc.scalar.activation(edge_b[:, par, :, :], log_adj[:, par, :, :], ACT.Ln, bias=zero_col[:, :])\
                        .then_inc(log_done, 1)
                    return
                wait(act, edge_done, 2 * (t - 1))
                nc.scalar.activation(log_adj[:, par, :, :].rearrange("p j n -> p (j n)"),
                                     ADJ[:, bass.ds(t * PN, PN)], ACT.Ln, bias=eps_col[:, :])\
                    .then_inc(log_done, 1)

            def high_out(act, pair, j):
                act.wait_ge(pv_ready, 2 * pair + j + 1)
                wait(act, y_ready, pair)
                nc.scalar.copy(oT_hi[:, :, j * N:(j + 1) * N], PV[:, 0:D].rearrange("p (m n) -> p m n", m=KT))\
                    .then_inc(ot_hi, 1)

            def act_step(t, par):
                act = nc.scalar
                a, b, bp = 2 * (t - 1), 2 * (t - 1) + 1, 2 * (t - 1) - 1
                proj = within(t, 0, PAIRS)
                here = within(t, 1, PAIRS + 1)
                last = within(t, 2, PAIRS + 2)
                more = within(t, -1, PAIRS - 1)
                if normed:
                    if proj:
                        evac_q(act, t, par)
                    if here:
                        exps(act, a, 0, 0)
                        exps(act, a, 0, 1)
                    if last:
                        high_out(act, t - 2, 0)
                        evac_att(act, bp, 1)
                    if proj:
                        log_edges(act, t, par)
                    if more:
                        evac_x(act, t + 1, 1 - par)
                    if last:
                        high_out(act, t - 2, 1)
                    if proj:
                        evac_v(act, t, par)
                    if here:
                        evac_att(act, a, 0)
                        exps(act, b, 1, 0)
                        exps(act, b, 1, 1)
                else:
                    if proj:
                        evac_q(act, t, par)
                    if here:
                        exps(act, a, 0, 0)
                    if proj:
                        evac_nodes(act, t, par)
                        log_edges(act, t, par)
                    if here:
                        exps(act, a, 0, 1)
                    if last:
                        evac_att(act, bp, 1)
                    if proj:
                        evac_v(act, t, par)
                    if more:
                        evac_x(act, t + 1, 1 - par)
                    if here:
                        evac_att(act, a, 0)
                        exps(act, b, 1, 0)
                        exps(act, b, 1, 1)

            def act_prog(act):
                if not layer:
                    start(act)
                evac_x(act, 0, 0)
                if normed:
                    act_step(0, 0)
                    scalar_prep_rest(act)
                steps(act, 1 if normed else 0, PAIRS + 1, 4, PAIRS - 2, act_step)
            progs["scalar"].append(act_prog)

            def add_edges(dve, g, j, pair, epar):
                dve.wait_ge(s_ready, g + 1)
                if normed:
                    dve.wait_ge(log_done, pair + 1)
                else:
                    dve.wait_ge(edge_done, g + 1)
                wait(dve, at_ready, g - 1)
                nc.vector.tensor_tensor(att[:, j, :, :], SC[:, :, :],
                                        edge_b[:, epar, j, :].unsqueeze(1).broadcast_to([P, H, N]),
                                        ALU.add).then_inc(sum_done, 1)

            def head_max(dve, g, j):
                wait(dve, exp_half, 2 * (g - 1))
                dve.wait_ge(sum_done, g + 1)
                nc.vector.tensor_reduce(negmax[:, j, :], att[:, j, :, :], AX.X, ALU.max, negate=True)\
                    .then_inc(max_done, 1)

            def edge_bias(dve, t, par):
                dve.wait_ge(kb_ready, t + 1)
                dve.wait_ge(log_done, t + 1)
                wait(dve, sum_done, 2 * (t - 1))
                for j in range(2):
                    nc.vector.scalar_tensor_tensor(edge_b[:, par, j, :], VB[j][:, 3 * N:4 * N],
                                                   node_b[:, par, j, 0:1], log_adj[:, par, j, :],
                                                   ALU.add, ALU.add).then_inc(edge_done, 1)

            def clip_adj(dve, t, par):
                wait(dve, log_done, t - 1)
                nc.vector.tensor_scalar(log_adj[:, par, :, :].rearrange("p j n -> p (j n)"),
                                        ADJ[:, bass.ds(t * PN, PN)], ADJ_MIN, None, ALU.max)\
                    .then_inc(adj_ready, 1)

            def reciprocals(dve, g, j, hf=0):
                if normed:
                    wait(dve, scale_half, 2 * (g - 1))
                    dve.wait_ge(exp_half, 2 * g + 1 + hf)
                    part = slice(hf * HPT, (hf + 1) * HPT)
                else:
                    wait(dve, norm_done, g - 1)
                    dve.wait_ge(exp_half, 2 * g + 2)
                    part = slice(0, H)
                nc.vector.reciprocal(rsum[:, j, part], asum[:, j, part]).then_inc(rec_done, 1)

            def low_out(dve, pair, j):
                dve.wait_ge(ot_hi, 2 * pair + j + 1)
                nc.vector.tensor_tensor(oT_lo[:, :, j * N:(j + 1) * N], PV[:, 0:D].rearrange("p (m n) -> p m n", m=KT),
                                        oT_hi[:, :, j * N:(j + 1) * N].bitcast(FP32),
                                        ALU.subtract).then_inc(ot_lo, 1)

            def copy_out(dve, g, j):
                dve.wait_ge(pv_ready, g + 1)
                wait(dve, back_ready, g - 1)
                nc.vector.tensor_copy(oT[:, :, j * N:(j + 1) * N],
                                      PV[:, 0:D].rearrange("p (m n) -> p m n", m=KT)).then_inc(copied, 1)

            def finish(dve, g, j):
                wait(dve, back_ready, g + 1)
                wait(dve, rec_done, g + 1)
                wait(dve, final, g - 1)
                nc.vector.tensor_tensor(onorm[:, j, :].rearrange("p (h d) -> p h d", h=H),
                                        OB[j].rearrange("p (h d) -> p h d", h=H),
                                        rsum[:, j, :].unsqueeze(2).broadcast_to([P, H, DK]),
                                        ALU.mult).then_inc(norm_done, 1)

            def low_x(dve, i, par):
                dve.wait_ge(xt_hi, i + 1)
                nc.vector.tensor_tensor(xT_lo[:, par, :, :], XO[:, :].rearrange("p (k n) -> p k n", k=KT),
                                        xT_hi[:, par, :, :].bitcast(FP32), ALU.subtract).then_inc(xt_lo, 1)

            def residual(dve, pair):
                dve.wait_ge(y_ready, pair + 1)
                for j in range(2):
                    g = 2 * pair + j
                    wait(dve, final, g - 1)
                    nc.vector.tensor_tensor(yres[:, j, :], XO[:, j * D:(j + 1) * D],
                                            X[:, bass.ds(g * D, D)], ALU.add).then_inc(res_done, 1)

            def moments(dve, pair):
                for j in range(2):
                    g = 2 * pair + j
                    dve.wait_ge(res_done, g + 1)
                    nc.vector.bn_stats(stats[:, j, :], yres[:, j, :]).then_inc(st_done, 1)

            def aggregate_waits(dve, pair):
                dve.wait_ge(st_done, 2 * pair + 2)
                wait(dve, z_done, 2 * pair)
                wait(dve, ve_done, 2 * pair)

            def aggregate(dve, pair):
                for j in range(2):
                    nc.vector.bn_aggr(mv[:, j, :], stats[:, j, :]).then_inc(mv_done, 1)

            def center(dve, pair):
                for j in range(2):
                    g = 2 * pair + j
                    dve.wait_ge(mv_done, g + 1)
                    nc.vector.scalar_tensor_tensor(yres[:, j, :], yres[:, j, :], mv[:, j, 0:1], gamma_b[:, :],
                                                   ALU.subtract, ALU.mult).then_inc(z_done, 1)

            def scale_shift(dve, pair):
                for j in range(2):
                    g = 2 * pair + j
                    dve.wait_ge(z_done, g + 1)
                    dve.wait_ge(rstd_done, g + 1)
                    nc.vector.scalar_tensor_tensor(X[:, bass.ds(g * D, D)], yres[:, j, :], rstd[:, j, :],
                                                   beta_b[:, :], ALU.mult, ALU.add).then_inc(final, 1)

            def evac_k(dve, t, par):
                dve.wait_ge(k_ready, t + 1)
                wait(dve, s_ready, 2 * (t - 1))
                for m in range(KT):
                    ins = nc.vector.scalar_tensor_tensor(
                        KBD[:, par, m, :, :], QK[:, m * PN:(m + 1) * PN].unsqueeze(1).broadcast_to([P, HPR, PN]),
                        bcol[:, ck, m:m + 1], block_mask[:, :].unsqueeze(2).broadcast_to([P, HPR, PN]),
                        ALU.add, ALU.mult)
                ins.then_inc(k_done, 1)

            def dve_step(t, par):
                dve = nc.vector
                a, b, bp = 2 * (t - 1), 2 * (t - 1) + 1, 2 * (t - 1) - 1
                proj = within(t, 0, PAIRS)
                here = within(t, 1, PAIRS + 1)
                last = within(t, 2, PAIRS + 2)
                oldest = within(t, 4, PAIRS + 4)
                older = within(t, 3, PAIRS + 3)
                more = within(t, -1, PAIRS - 1)
                if here:
                    add_edges(dve, a, 0, t - 1, 1 - par)
                if normed and last:
                    reciprocals(dve, bp, 1, 1)
                if here:
                    head_max(dve, a, 0)
                if normed:
                    if oldest:
                        scale_shift(dve, t - 4)
                    if older:
                        residual(dve, t - 3)
                        moments(dve, t - 3)
                        aggregate_waits(dve, t - 3)
                    if proj:
                        clip_adj(dve, t, par)
                    if older:
                        aggregate(dve, t - 3)
                    if here:
                        reciprocals(dve, a, 0, 0)
                    if older:
                        center(dve, t - 3)
                    if here:
                        reciprocals(dve, a, 0, 1)
                    if last:
                        low_out(dve, t - 2, 0)
                    if here:
                        add_edges(dve, b, 1, t - 1, 1 - par)
                    if proj:
                        evac_k(dve, t, par)
                    if here:
                        head_max(dve, b, 1)
                    if more:
                        low_x(dve, t + 1, 1 - par)
                    if last:
                        low_out(dve, t - 2, 1)
                    if here:
                        reciprocals(dve, b, 1, 0)
                else:
                    if last:
                        reciprocals(dve, bp, 1)
                        copy_out(dve, bp - 1, 0)
                        finish(dve, bp - 1, 0)
                    if here:
                        add_edges(dve, b, 1, t - 1, 1 - par)
                    if proj:
                        edge_bias(dve, t, par)
                        evac_k(dve, t, par)
                    if here:
                        reciprocals(dve, a, 0)
                    if last:
                        copy_out(dve, bp, 1)
                    if here:
                        head_max(dve, b, 1)
                    if more:
                        low_x(dve, t + 1, 1 - par)
                    if last:
                        finish(dve, bp, 1)

            def dve_prog(dve):
                if not layer:
                    start(dve)
                low_x(dve, 0, 0)
                if normed:
                    dve.wait_ge(load_adj[0], 16)
                    dve_step(0, 0)
                    vector_prep_rest(dve)
                steps(dve, 1 if normed else 0, PAIRS + 1 + 2 * normed, 4, PAIRS - 2, dve_step)
            progs["vector"].append(dve_prog)

            return xt_ready, res_done if normed else norm_done

        def masked_layer(layer, before):
            L = f"{layer}"
            w = slot(W_SLOTS, "fc" + L)
            br = slot(B_SLOTS, "fc" + L)
            staged = [sem(f"staged{L}_{p}") for p in range(2)]
            xt_ready, xt_hi, xt_lo = sem("xt_ready" + L), sem("xt_hi" + L), sem("xt_lo" + L)
            v_ready, v_done = sem("v_ready" + L), sem("v_done" + L)
            kb_ready, logit_done, leaky_done = sem("kb_ready" + L), sem("logit_done" + L), sem("leaky_done" + L)
            max_done, exp_done, mask_ready = sem("max_done" + L), sem("exp_done" + L), sem("mask_ready" + L)
            pt_ready, pt_done, pv_ready, rec_done = (sem(n + L) for n in ("pt_ready", "pt_done", "pv_ready", "rec_done"))
            final = xfinal[layer]
            VB = [[QK[:, :], VY[:, :]], [SC[:, HPT:, :].rearrange("p h n -> p (h n)"), AT[:, HPT:, :].rearrange("p h n -> p (h n)")]]
            KB = SC[:, 0:2, :]
            PT = AT[:, 0:2, :]

            def start(eng):
                eng.wait_ge(before[1], B)
                eng.wait_ge(prepared_rest, PREPARED_REST)
                eng.wait_ge(rest_rows, REST_ROWS)

            def sync_prog(sp):
                sp.wait_ge(before[0], PAIRS)
                stage_x(sp, layer, staged, xt_ready)
            progs["sync"].append(sync_prog)

            def transpose_x(pe, i, par):
                pe.wait_ge(staged[par], 8 * (i - par) + 16)
                wait(pe, xt_lo, i)
                for k in range(KT):
                    for j in range(2):
                        mm = nc.tensor.transpose(XO[:, k * PN + j * N:k * PN + (j + 1) * N],
                                                 xin[:, par, j, k * P:(k + 1) * P], ident[:, :])
                mm.then_inc(xt_ready, 1)

            def pe_step(t, par):
                pe = nc.tensor
                if within(t, 0, PAIRS):
                    pe.wait_ge(xt_hi, t + 1)
                    pe.wait_ge(xt_lo, t + 1)
                    wait(pe, v_done, t - 1)
                    for j in range(2):
                        mm = projected(VB[par][j][:, 0:DX], t, j, w, br, DX, par)
                    mm.then_inc(v_ready, 1)
                if within(t, 2, PAIRS + 2):
                    pe.wait_ge(exp_done, 2 * (t - 1))
                    wait(pe, pt_done, t - 2)
                    for j in range(2):
                        mm = nc.tensor.transpose(PT[:, j, :], prob[:, j, :], ident[:, :])
                    mm.then_inc(pt_ready, 1)
                if within(t, 1, PAIRS + 1):
                    pe.wait_ge(v_done, t)
                    wait(pe, logit_done, 2 * (t - 1))
                    for j in range(2):
                        mm = nc.tensor.transpose(KB[:, j, :], VX[:, 1 - par, j, D + 1:D + 2].broadcast_to([P, P]),
                                                 ident[:, :])
                    mm.then_inc(kb_ready, 1)
                if within(t, -2, PAIRS - 2):
                    transpose_x(pe, t + 2, par)
                if within(t, 2, PAIRS + 2):
                    pe.wait_ge(pt_done, t - 1)
                    wait(pe, final, 2 * (t - 2))
                    for j in range(2):
                        mm = nc.tensor.matmul(PV[:, j * D:(j + 1) * D], probT[:, j, :],
                                              VX[:, par, j, 0:D], start=True, stop=True)
                    mm.then_inc(pv_ready, 1)

            def pe_prog(pe):
                start(pe)
                transpose_x(pe, 0, 0)
                transpose_x(pe, 1, 1)
                steps(pe, 0, PAIRS + 1, 4, PAIRS - 2, pe_step)
            progs["tensor"].append(pe_prog)

            def evac_x(act, i, par):
                act.wait_ge(xt_ready, i + 1)
                wait(act, v_ready, i - 1)
                nc.scalar.copy(xT_hi[:, par, :, :], XO[:, :].rearrange("p (k n) -> p k n", k=KT))\
                    .then_inc(xt_hi, 1)

            def act_step(t, par):
                act = nc.scalar
                if within(t, 2, PAIRS + 2):
                    act.wait_ge(pt_ready, t - 1)
                    wait(act, pv_ready, t - 2)
                    nc.scalar.copy(probT, PT).then_inc(pt_done, 1)
                if within(t, -2, PAIRS - 2):
                    evac_x(act, t + 2, par)
                if within(t, 0, PAIRS):
                    act.wait_ge(v_ready, t + 1)
                    wait(act, pv_ready, t - 1)
                    for j in range(2):
                        ins = nc.scalar.copy(VX[:, par, j, :], VB[par][j][:, 0:DX])
                    ins.then_inc(v_done, 1)
                if within(t, 1, PAIRS + 1):
                    act.wait_ge(max_done, t)
                    wait(act, pt_ready, t - 1)
                    wait(act, rec_done, t - 1)
                    for j in range(2):
                        nc.scalar.activation(prob[:, j, :], leaky[:, j, :], ACT.Exp, bias=nmax1[:, j:j + 1],
                                             accum_out=psum1[:, j:j + 1]).then_inc(exp_done, 1)

            def act_prog(act):
                evac_x(act, 0, 0)
                evac_x(act, 1, 1)
                steps(act, 0, PAIRS + 1, 4, PAIRS - 2, act_step)
            progs["scalar"].append(act_prog)

            def low_x(dve, i, par):
                dve.wait_ge(xt_hi, i + 1)
                nc.vector.tensor_tensor(xT_lo[:, par, :, :], XO[:, :].rearrange("p (k n) -> p k n", k=KT),
                                        xT_hi[:, par, :, :].bitcast(FP32), ALU.subtract).then_inc(xt_lo, 1)

            def dve_step(t, par):
                dve = nc.vector
                if within(t, 1, PAIRS + 1):
                    wait(dve, logit_done, 2 * (t - 1))
                    nc.vector.tensor_scalar(mbias.rearrange("p j n -> p (j n)"),
                                            ADJ[:, bass.ds((t - 1) * PN, PN)], -1.0, MASKED, ALU.add, ALU.mult)\
                        .then_inc(mask_ready, 1)
                    dve.wait_ge(kb_ready, t)
                    dve.wait_ge(mask_ready, t)
                    wait(dve, leaky_done, t - 1)
                    for j in range(2):
                        nc.vector.scalar_tensor_tensor(logit[:, j, :], KB[:, j, :], VX[:, 1 - par, j, D:D + 1],
                                                       mbias[:, j, :], ALU.add, ALU.add).then_inc(logit_done, 1)
                    dve.wait_ge(logit_done, 2 * t)
                    wait(dve, exp_done, 2 * (t - 1))
                    nc.vector.scalar_tensor_tensor(leaky, logit, LEAKY, logit, ALU.mult, ALU.max)\
                        .then_inc(leaky_done, 1)
                    dve.wait_ge(leaky_done, t)
                    nc.vector.tensor_reduce(nmax1[:, :], leaky, AX.X, ALU.max, negate=True).then_inc(max_done, 1)
                if within(t, -2, PAIRS - 2):
                    low_x(dve, t + 2, par)
                if within(t, 2, PAIRS + 2):
                    dve.wait_ge(pv_ready, t - 1)
                    dve.wait_ge(rec_done, t - 1)
                    for j in range(2):
                        xg = X[:, bass.ds((2 * (t - 2) + j) * D, D)]
                        nc.vector.scalar_tensor_tensor(xg, PV[:, j * D:(j + 1) * D], prec[:, par, j:j + 1], xg,
                                                       ALU.mult, ALU.add).then_inc(final, 1)
                if within(t, 1, PAIRS + 1):
                    dve.wait_ge(exp_done, 2 * t)
                    wait(dve, final, 2 * (t - 2))
                    nc.vector.reciprocal(prec[:, 1 - par, :], psum1[:, :]).then_inc(rec_done, 1)

            def dve_prog(dve):
                low_x(dve, 0, 0)
                low_x(dve, 1, 1)
                steps(dve, 0, PAIRS + 1, 4, PAIRS - 2, dve_step)
            progs["vector"].append(dve_prog)
            return xt_ready, final

        progs["sync"].append(sync_prep)
        progs["scalar"].append(scalar_prep)
        progs["gpsimd"].append(gpsimd_prep)
        progs["vector"].append(vector_prep)
        before = attention(0)
        before = masked_layer(1, before)
        before = attention(2, before)
        masked_layer(3, before)
        progs["sync"].append(lambda sp: sp.wait_ge(stored, 16 * PAIRS))

        @block.sync
        def _(sp):
            for part in progs["sync"]:
                part(sp)

        @block.gpsimd
        def _(pool):
            for part in progs["gpsimd"]:
                part(pool)

        @block.scalar
        def _(act):
            for part in progs["scalar"]:
                part(act)

        @block.tensor
        def _(pe):
            for part in progs["tensor"]:
                part(pe)

        @block.vector
        def _(dve):
            for part in progs["vector"]:
                part(dve)


def kernel(**inputs):
    import numpy as np
    import concourse.bacc as bacc
    from concourse.bass_utils import run_bass_kernel_spmd

    a = {k: np.asarray(v) for k, v in inputs.items()}

    def tiles(w):
        return w.reshape(2, 128, -1).transpose(1, 0, 2)

    fwd = [a["L0_gnn_Wq"].T, a["L0_gnn_Wk"].T, a["L0_gnn_Wv"].T, a["L0_gnn_Wo"].T, a["L1_gnn_fc_w"].T,
           a["L2_gnn_W_q"], a["L2_gnn_W_k"], a["L2_gnn_W_v"], a["L3_gnn_W_fc"]]
    rev = [a["L1_gnn_fc_w"], a["L3_gnn_W_fc"].T]
    qkw = [np.stack([a["L1_gnn_q_w"][0], a["L1_gnn_k_w"][0]], 1),
           np.concatenate([a["L3_gnn_w_q"], a["L3_gnn_w_k"]], 1)]
    cols = [a[n] for n in ("L0_gnn_bq", "L0_gnn_bk", "L2_gnn_b_q", "L2_gnn_b_k", "L1_gnn_fc_b", "L3_gnn_b_fc")]
    rows = [a[n] for n in ("L0_gnn_bv", "L0_gnn_bo", "L1_gnn_fc_b", "L2_gnn_b_v", "L3_gnn_b_fc")]
    arrays = {
        "x": a["x"], "adj": a["adj"],
        "weights": np.stack([tiles(w) for w in fwd], 1),
        "fc_rev": np.stack([tiles(w) for w in rev], 1),
        "qk_w": np.stack([tiles(w) for w in qkw], 1),
        "bias_cols": np.stack([tiles(c)[:, :, 0] for c in cols], 1),
        "bias_rows": np.stack(rows, 0),
        "qk_b": np.stack([np.concatenate([a["L1_gnn_q_b"], a["L1_gnn_k_b"]]),
                          np.concatenate([a["L3_gnn_b_q"], a["L3_gnn_b_k"]])], 0),
        "gamma": a["L0_gnn_gamma"], "beta": a["L0_gnn_beta"],
        "w_g": tiles(a["L2_gnn_w_g"].reshape(2, D).T), "b_g": a["L2_gnn_b_g"].reshape(1),
        "eye": np.eye(128, dtype=np.float32),
    }
    nc = bacc.Bacc("TRN2", target_bir_lowering=False, num_devices=1)
    arrays = {"in_" + k: np.ascontiguousarray(v) for k, v in arrays.items()}
    args = [nc.dram_tensor(k, v.shape, mybir.dt.from_np(v.dtype), kind="ExternalInput").ap()
            for k, v in arrays.items()]
    out = nc.dram_tensor("out", [B, N, D], FP32, kind="ExternalOutput").ap()
    build(nc, *args, out)
    r = run_bass_kernel_spmd(nc, [arrays], core_ids=[0])
    return r.results[0]["out"]
```
